# Optimizing a Trainium2 kernel written in Bass

```python
import numpy as np
import jax
import jax.numpy as jnp

def _softmax(x, axis=-1):
    return jax.nn.softmax(x, axis=axis)

def _gelu(x):
    return jax.nn.gelu(x, approximate=True)

def _silu(x):
    return jax.nn.silu(x)

def _sigmoid(x):
    return jax.nn.sigmoid(x)

def _layernorm(x, axis=-1, eps=1e-05):
    m = jnp.mean(x, axis=axis, keepdims=True)
    v = jnp.var(x, axis=axis, keepdims=True)
    return (x - m) / jnp.sqrt(v + eps)

def _scatter_add(tgt, idx, src, axis=0):
    return tgt.at[idx].add(src)

def _segment_sum(src, seg, n):
    return jax.ops.segment_sum(src, seg, n)
kernel_name = 'mk_conv_preact_d2_conv_nchw256_r2_e0f8a0'

def setup_inputs(seed: int=0):
    np.random.seed(seed)
    _w = jnp.asarray

    def _rec_inputs():
        import jax
        import jax.numpy as jnp
        _gk = jax.random.key(seed)
        x = -0.0002928 + 1 * jax.random.normal(jax.random.fold_in(_gk, 1), (4, 128, 32, 32), jnp.float32)
        return x
    x = _rec_inputs()

    def _L0_conv_setup():
        import jax, jax.numpy as jnp
        import numpy as np
        K = 3
        STRIDE = 1
        PAD = 1
        GROUPS = 16
        EPS = 1e-05

        def _conv2d(x, w, b, stride, pad):
            out = jax.lax.conv_general_dilated(x, w, (stride, stride), [(pad, pad), (pad, pad)], dimension_numbers=('NCHW', 'OIHW', 'NCHW'))
            return out + b[None, :, None, None]
        key = jax.random.key(seed)
        ks = jax.random.split(key, 6)
        B, Cin, H, W = (4, 128, 32, 32)
        Cout = 128
        x = jax.random.normal(ks[0], (B, Cin, H, W), dtype=jnp.float32)
        w_off = jax.random.normal(ks[1], (3 * K * K, Cin, K, K), dtype=jnp.float32) * 0.01
        b_off = jnp.zeros((3 * K * K,), dtype=jnp.float32)
        weight = jax.random.normal(ks[2], (Cout, Cin, K, K), dtype=jnp.float32) * 0.02
        bias = jnp.zeros((Cout,), dtype=jnp.float32)
        gamma = jnp.ones((Cout,), dtype=jnp.float32)
        beta = jnp.zeros((Cout,), dtype=jnp.float32)
        return {'x': x, 'w_off': w_off, 'b_off': b_off, 'weight': weight, 'bias': bias, 'gamma': gamma, 'beta': beta}
    _L0_conv_all = _L0_conv_setup()
    _L0_conv_in = {k: v for k, v in _L0_conv_all.items() if k in ('w_off', 'b_off', 'weight', 'bias', 'gamma', 'beta')}
    del _L0_conv_all

    def _L1_conv_setup():
        import jax, jax.numpy as jnp
        import numpy as np
        EPS = 1e-05

        def ternary_quantize(w):
            w = w - w.mean()
            mx, mn = (w.max(), w.min())
            third = (mx - mn) / 3
            lo = mn + third
            hi = mx - third
            return jnp.where(w < lo, -1.0, jnp.where(w > hi, 1.0, 0.0)).astype(w.dtype)

        def conv3x3(x, w):
            return jax.lax.conv_general_dilated(x, w, window_strides=(1, 1), padding=((1, 1), (1, 1)), dimension_numbers=('NCHW', 'OIHW', 'NCHW'))

        def batchnorm(x, gamma, beta):
            m = x.mean(axis=(0, 2, 3), keepdims=True)
            v = x.var(axis=(0, 2, 3), keepdims=True)
            xn = (x - m) * jax.lax.rsqrt(v + EPS)
            return xn * gamma.reshape(1, -1, 1, 1) + beta.reshape(1, -1, 1, 1)
        key = jax.random.key(seed)
        ks = jax.random.split(key, 3)
        N, C, H, W = (32, 128, 56, 56)
        x = jax.random.normal(ks[0], (N, C, H, W), dtype=jnp.float32)
        std = 1.0 / np.sqrt(C * 9)
        w1 = jax.random.normal(ks[1], (C, C, 3, 3), dtype=jnp.float32) * std
        w2 = jax.random.normal(ks[2], (C, C, 3, 3), dtype=jnp.float32) * std
        gamma1 = jnp.ones((C,), jnp.float32)
        beta1 = jnp.zeros((C,), jnp.float32)
        gamma2 = jnp.ones((C,), jnp.float32)
        beta2 = jnp.zeros((C,), jnp.float32)
        return {'x': x, 'w1': w1, 'gamma1': gamma1, 'beta1': beta1, 'w2': w2, 'gamma2': gamma2, 'beta2': beta2}
    _L1_conv_all = _L1_conv_setup()
    _L1_conv_in = {k: v for k, v in _L1_conv_all.items() if k in ('w1', 'gamma1', 'beta1', 'w2', 'gamma2', 'beta2')}
    del _L1_conv_all
    return {'x': x, 'L0_conv_w_off': _L0_conv_in['w_off'], 'L0_conv_b_off': _L0_conv_in['b_off'], 'L0_conv_weight': _L0_conv_in['weight'], 'L0_conv_bias': _L0_conv_in['bias'], 'L0_conv_gamma': _L0_conv_in['gamma'], 'L0_conv_beta': _L0_conv_in['beta'], 'L1_conv_w1': _L1_conv_in['w1'], 'L1_conv_gamma1': _L1_conv_in['gamma1'], 'L1_conv_beta1': _L1_conv_in['beta1'], 'L1_conv_w2': _L1_conv_in['w2'], 'L1_conv_gamma2': _L1_conv_in['gamma2'], 'L1_conv_beta2': _L1_conv_in['beta2']}

def reference(x, L0_conv_w_off, L0_conv_b_off, L0_conv_weight, L0_conv_bias, L0_conv_gamma, L0_conv_beta, L1_conv_w1, L1_conv_gamma1, L1_conv_beta1, L1_conv_w2, L1_conv_gamma2, L1_conv_beta2):
    import jax
    import jax.numpy as jnp

    def _L0_conv_ref(x, w_off, b_off, weight, bias, gamma, beta):
        import jax, jax.numpy as jnp
        import numpy as np
        K = 3
        STRIDE = 1
        PAD = 1
        GROUPS = 16
        EPS = 1e-05

        def _conv2d(x, w, b, stride, pad):
            out = jax.lax.conv_general_dilated(x, w, (stride, stride), [(pad, pad), (pad, pad)], dimension_numbers=('NCHW', 'OIHW', 'NCHW'))
            return out + b[None, :, None, None]
        B, Cin, H, W = x.shape
        Cout = weight.shape[0]
        KK = K * K
        om = _conv2d(x, w_off, b_off, STRIDE, PAD)
        Ho, Wo = (om.shape[2], om.shape[3])
        off_y, off_x, m = jnp.split(om, 3, axis=1)
        mask = jax.nn.sigmoid(m)
        kgy = jnp.repeat(jnp.arange(K, dtype=x.dtype), K)
        kgx = jnp.tile(jnp.arange(K, dtype=x.dtype), K)
        base_y = jnp.arange(Ho, dtype=x.dtype) * STRIDE - PAD
        base_x = jnp.arange(Wo, dtype=x.dtype) * STRIDE - PAD
        py = base_y[None, None, :, None] + kgy[None, :, None, None] + off_y
        px = base_x[None, None, None, :] + kgx[None, :, None, None] + off_x
        y0 = jnp.floor(py)
        x0 = jnp.floor(px)
        wy1 = py - y0
        wx1 = px - x0

        def gather(img, yy, xx):
            return img[:, yy, xx]

        def corner(yi, xi, wy, wx):
            valid = (yi >= 0) & (yi < H) & (xi >= 0) & (xi < W)
            yc = jnp.clip(yi, 0, H - 1).astype(jnp.int32)
            xc = jnp.clip(xi, 0, W - 1).astype(jnp.int32)
            vals = jax.vmap(gather)(x, yc, xc)
            w_ = (wy * wx * valid.astype(x.dtype))[:, None]
            return vals * w_
        sampled = corner(y0, x0, 1 - wy1, 1 - wx1) + corner(y0, x0 + 1, 1 - wy1, wx1) + corner(y0 + 1, x0, wy1, 1 - wx1) + corner(y0 + 1, x0 + 1, wy1, wx1)
        sampled = sampled * mask[:, None]
        out = jnp.einsum('bckhw,ock->bohw', sampled, weight.reshape(Cout, Cin, KK)) + bias[None, :, None, None]
        og = out.reshape(B, GROUPS, Cout // GROUPS, Ho, Wo)
        mu = og.mean(axis=(2, 3, 4), keepdims=True)
        var = og.var(axis=(2, 3, 4), keepdims=True)
        og = (og - mu) * jax.lax.rsqrt(var + EPS)
        out = og.reshape(B, Cout, Ho, Wo) * gamma[None, :, None, None] + beta[None, :, None, None]
        return out

    def _L1_conv_ref(x, w1, gamma1, beta1, w2, gamma2, beta2):
        import jax, jax.numpy as jnp
        import numpy as np
        EPS = 1e-05

        def ternary_quantize(w):
            w = w - w.mean()
            mx, mn = (w.max(), w.min())
            third = (mx - mn) / 3
            lo = mn + third
            hi = mx - third
            return jnp.where(w < lo, -1.0, jnp.where(w > hi, 1.0, 0.0)).astype(w.dtype)

        def conv3x3(x, w):
            return jax.lax.conv_general_dilated(x, w, window_strides=(1, 1), padding=((1, 1), (1, 1)), dimension_numbers=('NCHW', 'OIHW', 'NCHW'))

        def batchnorm(x, gamma, beta):
            m = x.mean(axis=(0, 2, 3), keepdims=True)
            v = x.var(axis=(0, 2, 3), keepdims=True)
            xn = (x - m) * jax.lax.rsqrt(v + EPS)
            return xn * gamma.reshape(1, -1, 1, 1) + beta.reshape(1, -1, 1, 1)
        q1 = ternary_quantize(w1)
        out1 = jax.nn.relu(batchnorm(conv3x3(x, q1), gamma1, beta1))
        q2 = ternary_quantize(w2)
        out2 = batchnorm(conv3x3(out1, q2), gamma2, beta2)
        return jax.nn.relu(out1 + out2)

    def _gn(v, G=32, eps=1e-05):
        B_, C_, H_, W_ = v.shape
        g = v.reshape(B_, G, C_ // G, H_, W_)
        m = jnp.mean(g, axis=(2, 3, 4), keepdims=True)
        s = jnp.var(g, axis=(2, 3, 4), keepdims=True)
        return ((g - m) / jnp.sqrt(s + eps)).reshape(v.shape)

    def _ln_c(v, eps=1e-06):
        m = jnp.mean(v, axis=1, keepdims=True)
        s = jnp.var(v, axis=1, keepdims=True)
        return (v - m) / jnp.sqrt(s + eps)

    def _ln_t(v, eps=1e-05):
        m = jnp.mean(v, axis=-1, keepdims=True)
        s = jnp.var(v, axis=-1, keepdims=True)
        return (v - m) / jnp.sqrt(s + eps)

    def _to_tokens(v):
        B_, C_, H_, W_ = v.shape
        return v.reshape(B_, C_, H_ * W_).transpose(0, 2, 1)

    def _from_tokens(t, like):
        B_, C_, H_, W_ = like.shape
        return t.transpose(0, 2, 1).reshape(B_, C_, H_, W_)
    x = x + _L0_conv_ref(_gn(x), L0_conv_w_off, L0_conv_b_off, L0_conv_weight, L0_conv_bias, L0_conv_gamma, L0_conv_beta)
    x = x + _L1_conv_ref(_gn(x), L1_conv_w1, L1_conv_gamma1, L1_conv_beta1, L1_conv_w2, L1_conv_gamma2, L1_conv_beta2)
    return x

_drawn_inputs = setup_inputs


def setup_inputs(seed=0):
    import zlib

    import numpy as np

    out = dict(_drawn_inputs(seed))
    spreads = {'L0_conv_b_off': (0.0, 0.1),
     'L0_conv_bias': (0.0, 0.1),
     'L0_conv_gamma': (1.0, 0.2),
     'L0_conv_beta': (0.0, 0.1),
     'L1_conv_gamma1': (1.0, 0.2),
     'L1_conv_beta1': (0.0, 0.1),
     'L1_conv_gamma2': (1.0, 0.2),
     'L1_conv_beta2': (0.0, 0.1)}
    factors = {}
    for name, (base, spread) in spreads.items():
        noise = np.random.default_rng([zlib.crc32(name.encode()), seed]).standard_normal(out[name].shape)
        drawn = base * np.exp(spread * noise) if base else spread * noise
        out[name] = jnp.asarray(drawn.astype(out[name].dtype))
    for name, factor in factors.items():
        out[name] = (out[name] * factor).astype(out[name].dtype)
    return out
```

```python
from contextlib import ExitStack

import concourse.bass as bass
from concourse import mybir

F32 = mybir.dt.float32
F32R = mybir.dt.float32r
I32 = mybir.dt.int32
ALU = mybir.AluOpType
ACT = mybir.ActivationFunctionType
AX = mybir.AxisListType

B, C, H, W = 4, 128, 32, 32
P = 128
K = 3
TAPS = K * K
HW = H * W
TR = P // W
NT = HW // P
REACH = 2
WIN = 2 * TR
TOP = REACH + 1
ROWS = H + TR
PROWS = B * ROWS + 2
PW = W + 2
OFFC = 3 * TAPS
TAIL = 32
EPS = 1e-5
SLOTS = NT * K
ZPER = (NT + 1) * K
BIG = 512


def build(nc, x, w_off, b_off, wd, bias, gamma, beta, w1, g1, be1, w2, g2, be2, out):
    x_v = x.rearrange("b c h w -> c b (h w)")
    out_v = out.rearrange("b c h w -> c b (h w)")
    flat = "o c h w -> o (c h w)"

    with ExitStack() as ctx:
        def sb(name, shape, dt=F32):
            return ctx.enter_context(nc.sbuf_tensor(name, shape, dt))

        def ps(name, shape):
            return ctx.enter_context(nc.psum_tensor(name, shape, F32))

        def sem(name):
            return ctx.enter_context(nc.semaphore(name))

        xs = sb("xs", [P, B, HW])
        xhi = sb("xhi", [P, PROWS, PW], F32R)
        xlo = sb("xlo", [P, PROWS, PW], F32R)
        ysb = sb("ysb", [P, B, HW])
        colw = sb("colw", [P, B * NT, TAPS, W])
        roww = sb("roww", [P, B * NT, TAPS, WIN])
        woff_raw = sb("woff_raw", [OFFC, C * TAPS])
        wd_raw = sb("wd_raw", [P, C * TAPS])
        woffT = sb("woffT", [P, TAPS, P], F32R)
        wdhi = sb("wdhi", [P, TAPS, P], F32R)
        wdlo = sb("wdlo", [P, TAPS, P], F32R)
        q1 = sb("q1", [P, TAPS, P], F32R)
        q2 = sb("q2", [P, TAPS, P], F32R)
        omc = sb("omc", [2 * TAIL, 2, BIG])
        om2 = sb("om2", [P, B * NT, 2 * TAIL])
        om = sb("om", [P, B * NT, OFFC])
        xwin = sb("xwin", [P, 2, 2, K + TR - 1, W], F32R)
        zr = sb("zr", [P, 2, K, K, P])
        sT = sb("sT", [P, 2, K, WIN * W])
        sq = sb("sq", [P, 2, 2, K * P])
        ident = sb("ident", [P, P])
        g32 = sb("g32", [P, P])
        g16 = sb("g16", [P, P])
        boffb = sb("boffb", [P, OFFC])
        vec = sb("vec", [P, 8])
        ci = sb("ci", [P, 4], I32)
        cf = sb("cf", [P, 4])
        bxi = sb("bxi", [P, TAPS], I32)
        byi = sb("byi", [P, B * NT, TAPS], I32)
        bxf = sb("bxf", [P, TAPS])
        byf = sb("byf", [P, B * NT, TAPS])
        px = sb("px", [P, B * NT, TAPS])
        py = sb("py", [P, B * NT, TAPS])
        pyr = sb("pyr", [P, B * NT, TAPS])
        mask = sb("mask", [P, B * NT, TAPS])
        posany = sb("posany", [P, 2, NT])
        rowany = sb("rowany", [P, NT, H])
        st = sb("st", [P, 5, 2 * B, 6])
        mv = sb("mv", [P, 5, B, 2])
        nsm = sb("nsm", [P, 5, 10, B])
        tw = sb("tw", [P, 2, 16])
        far = sb("far", [P, 2])
        fari = sb("fari", [1, 1], I32)
        colf = colw[:, :, :, :].rearrange("p t k w -> p (t k w)")
        r1 = colf[:, 0:B * HW].rearrange("p (b n) -> p b n", b=B)
        tscr = colf[:, 0:C * TAPS]
        rowf = roww[:, :, :, :].rearrange("p t k w -> p (t k w)")
        wraw = [rowf[:, i * C * TAPS:(i + 1) * C * TAPS] for i in range(2)]
        zany = om2[:, 0:B * NT // 2, :].rearrange("p t n -> p (t n)")

        PS = ctx.enter_context(nc.psum_tensor("PS", [P, 2 * B, BIG], F32))
        S_PS = [PS[:, 0:2, :], PS[:, 2:4, :]]
        Z_PS = [PS[:, 4, :], PS[:, 5, :]]
        O_PS = [PS[:, 6, :], PS[:, 7, :]]

        x_in = [sem(f"x_in{b}") for b in range(B)]
        woff_in, wd_in, w1_in, w2_in, vec_in, boff_in = (
            sem(n) for n in ("woff_in", "wd_in", "w1_in", "w2_in", "vec_in", "boff_in"))
        gps = sem("gps")
        consts = sem("consts")
        dch = sem("dch")
        pads = sem("pads")
        gn_in, gn_mean, gn_dev, gn_msq, gn_var, gn_std = (
            sem(n) for n in ("gn_in", "gn_mean", "gn_dev", "gn_msq", "gn_var", "gn_std"))
        gn_ok = sem("gn_ok")
        xhi_ok, xlo_ok = sem("xhi_ok"), sem("xlo_ok")
        woff_t, woff_hi, woff_ok = sem("woff_t"), sem("woff_hi"), sem("woff_ok")
        wd_t, wd_hi, wd_ok = sem("wd_t"), sem("wd_hi"), sem("wd_ok")
        off_mm, off_cp, off_t, off_ok = (sem(n) for n in ("off_mm", "off_cp", "off_t", "off_ok"))
        om_ok, mask_ok = sem("om_ok"), sem("mask_ok")
        far_in, far_red, far_ok = sem("far_in"), sem("far_red"), sem("far_ok")
        tern_in, tern_red, tern_ok = sem("tern_in"), sem("tern_red"), sem("tern_ok")
        q_t, q_ok = sem("q_t"), sem("q_ok")
        dist_ok, abs_ok = sem("dist_ok"), sem("abs_ok")
        sT_ok, s_t, s_ok = sem("sT_ok"), sem("s_t"), sem("s_ok")
        xw_ok, z_mm, z_ok = sem("xw_ok"), sem("z_mm"), sem("z_ok")
        o_mm, y_ok = sem("o_mm"), sem("y_ok")
        any_ok = sem("any_ok")
        y_done = sem("y_done")
        y_norm, x1_ok = sem("y_norm"), sem("x1_ok")
        c1_mm, c2_mm = sem("c1_mm"), sem("c2_mm")
        r1_ok, r1hi_ok, r1lo_ok = sem("r1_ok"), sem("r1hi_ok"), sem("r1lo_ok")
        f_sum, f_relu, f_ok, out_done = (sem(n) for n in ("f_sum", "f_relu", "f_ok", "out_done"))

        CREDIT = 2
        GRP = 8
        GN0, GN8, GN1, BN1, BN2 = range(5)
        v_bias, v_gamma, v_beta, v_g1, v_be1, v_g2, v_be2 = (vec[:, i:i + 1] for i in range(7))

        def scale_of(n, b):
            return nsm[:, n, 8, b:b + 1]

        def shift_of(n, b):
            return nsm[:, n, 9, b:b + 1]

        def inner(img, b):
            return img[:, b * ROWS + TOP:b * ROWS + TOP + H, 1:1 + W]

        def square(a):
            return a.rearrange("p (h w) -> p h w", w=W)

        block = ctx.enter_context(nc.Block())

        @block.sync
        def _(sp):
            for b in range(B):
                sp.dma_start(xs[:, b, :], x_v[:, b, :]).then_inc(x_in[b], 16)
            sp.dma_start(wraw[0], w1.rearrange(flat)).then_inc(w1_in, 16)
            sp.dma_start(wraw[1], w2.rearrange(flat)).then_inc(w2_in, 16)
            for i, v in enumerate((bias, gamma, beta, g1, be1, g2, be2)):
                sp.dma_start(vec[:, i:i + 1], v.rearrange("(c a) -> c a", a=1)).then_inc(vec_in, 16)
            for n in range(2 * B):
                sp.wait_ge(f_ok, n + 1)
                sp.dma_start(out_v[:, n // 2, (n % 2) * BIG:(n % 2 + 1) * BIG],
                             ysb[:, n // 2, (n % 2) * BIG:(n % 2 + 1) * BIG]).then_inc(out_done, 16)
            sp.wait_ge(out_done, 16 * 2 * B)

        @block.gpsimd
        def _(pool):
            g = nc.gpsimd
            g.memset(ident[:, :], 1.0).then_inc(gps, 1)
            g.memset(g32[:, :], 0.25).then_inc(gps, 1)
            g.memset(g16[:, :], 0.125).then_inc(gps, 1)
            pool.wait_ge(gps, 3)
            g.affine_select(out=ident[:, :], in_=ident[:, :], compare_op=ALU.is_equal, fill=0.0, base=0,
                            pattern=[[-1, P]], channel_multiplier=1).then_inc(consts, 1)
            for m, n in ((g32, 4), (g16, 8)):
                v = m[:, :].rearrange("p (g n) -> p g n", n=n)
                g.affine_select(out=v, in_=v, compare_op=ALU.is_ge, fill=0.0, base=0,
                                pattern=[[-n, P // n], [0, n]], channel_multiplier=1).then_inc(gps, 1)
            pool.wait_ge(gps, 5)
            for m, n in ((g32, 4), (g16, 8)):
                v = m[:, :].rearrange("p (g n) -> p g n", n=n)
                g.affine_select(out=v, in_=v, compare_op=ALU.is_ge, fill=0.0, base=n - 1,
                                pattern=[[n, P // n], [0, n]], channel_multiplier=-1).then_inc(consts, 1)
            g.memset(xhi[:, :, :].bitcast(F32), 0.0).then_inc(pads, 1)
            g.iota(ci[:, 0:1], [[0, 1]], base=0, channel_multiplier=1).then_inc(consts, 1)
            g.iota(bxi[:, :], [[0, K], [1, K]], base=-1, channel_multiplier=1).then_inc(consts, 1)
            for b in range(B):
                g.iota(byi[:, b * NT:(b + 1) * NT, :], [[TR, NT], [1, K], [0, K]], base=-1,
                       channel_multiplier=0).then_inc(consts, 1)
            for i in range(2):
                pool.wait_ge(tern_in, i + 1)
                g.partition_all_reduce(tw[:, i, 4:5], tw[:, i, 0:1], P, bass.bass_isa.ReduceOp.add).then_inc(tern_red, 1)
                g.partition_all_reduce(tw[:, i, 5:7], tw[:, i, 1:3], P, bass.bass_isa.ReduceOp.max).then_inc(tern_red, 1)
            pool.wait_ge(far_in, 1)
            g.partition_all_reduce(far[:, 1:2], far[:, 0:1], P, bass.bass_isa.ReduceOp.max).then_inc(far_red, 1)

            pool.sem_inc(xw_ok, CREDIT)

            def window(row, rows, par):
                for part, src in enumerate((xhi, xlo)):
                    g.tensor_copy(xwin[:, part, par, 0:rows, :], src[:, bass.ds(row, rows), 1:1 + W]).then_inc(xw_ok, 1)

            pool.wait_ge(xhi_ok, B)
            pool.wait_ge(xlo_ok, B)
            pool.wait_ge(far_ok, 1)
            near = pool.value_load(fari[0:1, 0:1], min_val=0, max_val=1)
            with pool.If(near == 1):
                def near_window(b, j, par, done):
                    pool.wait_ge(z_mm, b * ZPER + done + CREDIT)
                    window(b * ROWS + j * TR, K + TR - 1, par)

                with pool.Fori(0, B) as b:
                    near_window(b, 0, 0, 0)
                    near_window(b, 1, 1, 0)
                    with pool.Fori(0, NT // 2 - 1) as i:
                        for par in range(2):
                            near_window(b, 2 * i + 2 + par, par, 6 * i + 3 * par + 3)
                    near_window(b, NT, 0, K * (NT - 1))
            with pool.Else():
                with pool.Fori(0, B) as b:
                    with pool.Fori(0, TAPS) as k:
                        for j in range(NT):
                            pool.wait_ge(z_mm, (b * TAPS + k) * NT + j - 1 + CREDIT)
                            window(b * ROWS + TOP + j * TR, TR, j % 2)

            for b in range(B):
                pool.wait_ge(y_norm, b + 1)
                g.tensor_tensor(xs[:, b, 0:256], xs[:, b, 0:256], ysb[:, b, 0:256], ALU.add).then_inc(x1_ok, 1)

        @block.tensor
        def _(pe):
            t = nc.tensor
            pe.wait_ge(consts, 3)
            pe.wait_ge(woff_in, 16)
            v = woff_raw[:, :].rearrange("o (c k) -> o k c", k=TAPS)
            for k in range(TAPS):
                last = t.transpose(PS[:, 0, k * OFFC:(k + 1) * OFFC], v[:, k, :], ident[0:OFFC, 0:OFFC])
            last.then_inc(woff_t, 1)
            pe.wait_ge(wd_in, 16)
            v = wd_raw[:, :].rearrange("o (c k) -> o k c", k=TAPS)
            for k in range(TAPS):
                last = t.transpose(PS[:, 1 + k // K, (k % K) * P:(k % K + 1) * P], v[:, k, :], ident[:, :])
                if k % K == K - 1:
                    last.then_inc(wd_t, 1)

            def group_sums(n, mat, m_ps, v_ps):
                pe.wait_ge(gn_in, n + 1)
                t.matmul(m_ps, mat[:, :], mv[:, (GN0, GN8, GN1)[n], :, 0], start=True, stop=True).then_inc(gn_mean, 1)
                pe.wait_ge(gn_dev, n + 1)
                t.matmul(v_ps, mat[:, :], nsm[:, (GN0, GN8, GN1)[n], 1, :], start=True, stop=True).then_inc(gn_msq, 1)

            group_sums(0, g32, O_PS[0][:, 0:B], O_PS[1][:, 0:B])

            def offset_half(b, h, wait_cp, wait_cp2):
                if wait_cp is not None:
                    pe.wait_ge(off_cp, wait_cp)
                for k in range(TAPS):
                    r = b * ROWS + TOP - 1 + h * (H // 2) + k // K
                    for part, src in enumerate((xhi, xlo)):
                        last = t.matmul(Z_PS[h], woffT[:, k, :], src[:, bass.ds(r, H // 2), k % K:k % K + W],
                                        start=(k == 0 and part == 0), stop=(k == TAPS - 1 and part == 1))
                last.then_inc(off_mm, 1)

            def offset_turn(n, h, wait_prev):
                pe.wait_ge(off_cp, n + 1)
                if wait_prev:
                    pe.wait_ge(off_ok, n - 1)
                for i in range(4):
                    last = t.transpose(O_PS[h][:, i * 2 * TAIL:(i + 1) * 2 * TAIL], omc[:, h, i * P:(i + 1) * P],
                                       ident[0:2 * TAIL, 0:2 * TAIL])
                last.then_inc(off_t, 1)

            pe.wait_ge(woff_ok, 1)
            pe.wait_ge(gn_ok, 1)
            for b in range(B):
                pe.wait_ge(xhi_ok, b + 1)
                pe.wait_ge(xlo_ok, b + 1)
                for h in range(2):
                    n = 2 * b + h
                    offset_half(b, h, n - 1 if n >= 2 else None, None)
                    if n >= 1:
                        offset_turn(n - 1, (n - 1) % 2, n - 1 >= 2)
            offset_turn(2 * B - 1, 1, True)

            pe.wait_ge(wd_hi, K)
            pe.wait_ge(wd_ok, K)
            for i in range(2):
                pe.wait_ge(tern_ok, i + 1)
                v = wraw[i].rearrange("o (c k) -> o k c", k=TAPS)
                for m in range(K):
                    if i:
                        pe.wait_ge(q_ok, m + 1)
                    for k in range(K * m, K * m + K):
                        last = t.transpose(PS[:, 1 + m, (k % K) * P:(k % K + 1) * P], v[:, k, :], ident[:, :])
                    last.then_inc(q_t, 1)
            pe.wait_ge(q_ok, 2 * K)
            pe.wait_ge(off_ok, 2 * B)

            for s in (s_t, z_mm, o_mm):
                pe.sem_inc(s, CREDIT)

            def z_block(bank, par, ky, w_taps):
                n = w_taps(wdhi)
                win = [xwin[:, part, par, ky:ky + TR, :].rearrange("p r w -> p (r w)") for part in range(2)]
                dst = Z_PS[bank][:, 0:n.shape[-1]]
                t.matmul(dst, win[0], n, start=True, stop=False)
                t.matmul(dst, win[1], n, start=False, stop=False)
                t.matmul(dst, win[0], w_taps(wdlo), start=False, stop=True).then_inc(z_mm, 1)

            pe.wait_ge(far_ok, 1)
            near = pe.value_load(fari[0:1, 0:1], min_val=0, max_val=1)
            with pe.If(near == 1):
                def turn(b, s, par):
                    pe.wait_ge(sT_ok, b * SLOTS + s + 1 + CREDIT)
                    pe.wait_ge(s_ok, b * SLOTS + s - 1 + CREDIT)
                    for kx in range(K):
                        for blk in range(2):
                            last = t.transpose(S_PS[par][:, blk, kx * P:(kx + 1) * P],
                                               sT[:, par, kx, blk * P:(blk + 1) * P], ident[:, :])
                    last.then_inc(s_t, 1)

                def make_z(b, j, z, par, ky, zpar, first):
                    if ky == 0:
                        pe.wait_ge(xw_ok, (b * (NT + 1) + j + 1) * 2 + CREDIT)
                    pe.wait_ge(z_ok, b * ZPER + z + (0 if first else -1) + CREDIT)
                    z_block(zpar, par, ky, lambda w: w[:, K * ky:K * ky + K, :].rearrange("p k o -> p (k o)"))

                def multiply(b, s, par, ky, spar, pt):
                    pe.wait_ge(s_ok, b * SLOTS + s + 1 + CREDIT)
                    pe.wait_ge(z_ok, b * ZPER + s + K + 1 + CREDIT)
                    if ky == 0:
                        pe.wait_ge(y_ok, b * NT + pt - 1 + CREDIT)
                    for kx in range(K):
                        for blk in range(2):
                            last = t.matmul(O_PS[par][:, 0:P], zr[:, (par + blk) % 2, ky, kx, :],
                                            sq[:, spar, blk, kx * P:(kx + 1) * P],
                                            start=(ky == 0 and kx == 0 and blk == 0),
                                            stop=(ky == K - 1 and kx == K - 1 and blk == 1))
                    last.then_inc(o_mm, 1)

                def pair(b, i, final):
                    for par in range(2):
                        for ky in range(K):
                            u = K * par + ky
                            s = 6 * i + u
                            if not (final and u == 5):
                                turn(b, s + 1, (u + 1) % 2)
                            if not (final and par == 1):
                                make_z(b, 2 * i + 2 + par, s + 6, par, ky, u % 2, False)
                            multiply(b, s, par, ky, u % 2, 2 * i + par)

                with pe.Fori(0, B) as b:
                    for j in range(2):
                        for ky in range(K):
                            make_z(b, j, K * j + ky, j, ky, (K * j + ky) % 2, j == 0 and ky == 0)
                    turn(b, 0, 0)
                    with pe.Fori(0, NT // 2 - 1) as i:
                        pair(b, i, False)
                    pair(b, NT // 2 - 1, True)
            with pe.Else():
                with pe.Fori(0, B) as b:
                    with pe.Fori(0, TAPS) as k:
                        it = b * TAPS + k
                        for j in range(NT):
                            pe.wait_ge(xw_ok, (it * NT + j + 1) * 2 + CREDIT)
                            pe.wait_ge(z_ok, it * NT + j - 1 + CREDIT)
                            z_block(j % 2, j % 2, 0, lambda w: w[:, bass.ds(k, 1), :].rearrange("p k o -> p (k o)"))
                        with pe.Fori(0, NT // 2) as i:
                            for par in range(2):
                                for half in range(2):
                                    n = (it * NT + 2 * i + par) * 2 + half
                                    pe.wait_ge(sT_ok, n + 1 + CREDIT)
                                    pe.wait_ge(s_ok, n - 1 + CREDIT)
                                    for j in range(4):
                                        last = t.transpose(S_PS[half][:, 0, j * P:(j + 1) * P],
                                                           sT[:, half, j // 2, (j % 2) * P:(j % 2 + 1) * P], ident[:, :])
                                    last.then_inc(s_t, 1)
                                pe.wait_ge(z_ok, (it + 1) * NT + CREDIT)
                                pe.wait_ge(y_ok, it * NT + 2 * i + par - 1 + CREDIT)
                                for j in range(NT):
                                    if j % 4 == 0:
                                        pe.wait_ge(s_ok, (it * NT + 2 * i + par) * 2 + j // 4 + 1 + CREDIT)
                                    last = t.matmul(O_PS[par][:, 0:P], zany[:, j * P:(j + 1) * P],
                                                    sq[:, j // 4, (j % 4) // 2, (j % 2) * P:(j % 2 + 1) * P],
                                                    start=(j == 0), stop=(j == NT - 1))
                                last.then_inc(o_mm, 1)

            group_sums(1, g16, Z_PS[0][:, 0:B], Z_PS[1][:, 0:B])
            group_sums(2, g32, S_PS[0][:, 0, 0:B], S_PS[1][:, 0, 0:B])
            pe.wait_ge(gn_ok, 3)

            def conv(q, b, done):
                for h in range(2):
                    for k in range(TAPS):
                        r = b * ROWS + TOP - 1 + h * (H // 2) + k // K
                        for part, src in enumerate((xhi, xlo)):
                            last = t.matmul(PS[:, bass.ds(2 * b + h, 1), :].rearrange("p a n -> p (a n)"), q[:, k, :],
                                            src[:, bass.ds(r, H // 2), k % K:k % K + W],
                                            start=(k == 0 and part == 0), stop=(k == TAPS - 1 and part == 1))
                    last.then_inc(done, 1)

            with pe.Fori(0, B) as b:
                pe.wait_ge(xhi_ok, B + b + 1)
                pe.wait_ge(xlo_ok, B + b + 1)
                conv(q1, b, c1_mm)
            with pe.Fori(0, B) as b:
                pe.wait_ge(r1hi_ok, 2 * b + 2)
                pe.wait_ge(r1lo_ok, 2 * b + 2)
                conv(q2, b, c2_mm)

        @block.scalar
        def _(act):
            a = nc.scalar
            act.dma_start(woff_raw[:, :], w_off.rearrange(flat)).then_inc(woff_in, 16)
            act.dma_start(wd_raw[:, :], wd.rearrange(flat)).then_inc(wd_in, 16)
            act.dma_start(boffb[:, :], b_off.partition_broadcast(P)).then_inc(boff_in, 16)
            act.wait_ge(woff_t, 1)
            act.wait_ge(pads, 3)
            a.activation(woffT[:, :, 0:OFFC], PS[:, 0, 0:TAPS * OFFC].rearrange("p (k o) -> p k o", k=TAPS),
                         ACT.Copy).then_inc(woff_hi, 1)

            def root(n):
                act.wait_ge(gn_var, n + 1)
                nb = 1 if n in (BN1, BN2) else B
                a.activation(nsm[:, n, 3, 0:nb], nsm[:, n, 2, 0:nb], ACT.Sqrt).then_inc(gn_std, 1)

            def heads(n, count):
                act.wait_ge(gn_ok, n + 1)
                for b in range(B):
                    a.activation(inner(xhi, b), square(xs[:, b, :]), ACT.Identity, bias=shift_of(n, b),
                                 scale=scale_of(n, b)).then_inc(xhi_ok, 1)

            root(GN0)
            heads(GN0, 0)
            for m in range(K):
                act.wait_ge(wd_t, m + 1)
                a.activation(wdhi[:, K * m:K * m + K, :], PS[:, 1 + m, 0:K * P].rearrange("p (k o) -> p k o", k=K),
                             ACT.Copy).then_inc(wd_hi, 1)
            def offset_tiles(n):
                act.wait_ge(off_t, n + 1)
                a.activation(om2[:, 4 * n:4 * n + 4, :], O_PS[n % 2][:, 0:8 * TAIL].rearrange("p (t o) -> p t o", t=4),
                             ACT.Copy).then_inc(off_ok, 1)

            for n in range(2 * B):
                act.wait_ge(off_mm, n + 1)
                if n >= 2:
                    act.wait_ge(off_t, n - 1)
                a.activation(omc[:, n % 2, :], Z_PS[n % 2][0:2 * TAIL, :], ACT.Copy).then_inc(off_cp, 1)
                if n >= 1:
                    offset_tiles(n - 1)
            offset_tiles(2 * B - 1)
            act.wait_ge(om_ok, 1)
            a.activation(mask[:, :, :], om[:, :, 2 * TAPS:OFFC], ACT.Sigmoid).then_inc(mask_ok, 1)
            for i, q in enumerate((q1, q2)):
                for m in range(K):
                    act.wait_ge(q_t, K * i + m + 1)
                    a.activation(q[:, K * m:K * m + K, :], PS[:, 1 + m, 0:K * P].rearrange("p (k o) -> p k o", k=K),
                                 ACT.Copy).then_inc(q_ok, 1)

            for n in range(W // GRP):
                act.wait_ge(dist_ok, n + 1)
                v = colw[:, :, :, n * GRP:(n + 1) * GRP]
                a.activation(v, v, ACT.Abs).then_inc(abs_ok, 1)
            act.wait_ge(dist_ok, W // GRP + 1)
            a.activation(rowf, rowf, ACT.Abs).then_inc(abs_ok, 1)

            for s in (s_ok, z_ok, y_ok):
                act.sem_inc(s, CREDIT)
            act.wait_ge(vec_in, 7 * 16)
            act.wait_ge(far_ok, 1)
            near = act.value_load(fari[0:1, 0:1], min_val=0, max_val=1)
            with act.If(near == 1):
                def copy_s(b, s, par):
                    act.wait_ge(s_t, b * SLOTS + s + 1 + CREDIT)
                    act.wait_ge(o_mm, b * SLOTS + s - 1 + CREDIT)
                    a.activation(sq[:, par, :, :], S_PS[par][:, :, 0:K * P], ACT.Copy).then_inc(s_ok, 1)

                def copy_z(b, z, par, ky, zpar, used):
                    act.wait_ge(z_mm, b * ZPER + z + 1 + CREDIT)
                    act.wait_ge(o_mm, b * SLOTS + used + CREDIT)
                    a.activation(zr[:, par, ky, :, :], Z_PS[zpar][:, 0:K * P].rearrange("p (k o) -> p k o", k=K),
                                 ACT.Copy).then_inc(z_ok, 1)

                def pair(b, i, final):
                    for par in range(2):
                        for ky in range(K):
                            u = K * par + ky
                            s = 6 * i + u
                            if not (final and u == 5):
                                copy_s(b, s + 1, (u + 1) % 2)
                            if not (final and par == 1):
                                copy_z(b, s + 6, par, ky, u % 2, s + 1)
                        act.wait_ge(o_mm, b * SLOTS + 6 * i + K * par + K + CREDIT)
                        a.activation(ysb[:, bass.ds(b, 1), bass.ds((2 * i + par) * P, P)].rearrange("p a n -> p (a n)"),
                                     O_PS[par][:, 0:P], ACT.Identity, bias=v_bias).then_inc(y_ok, 1)

                with act.Fori(0, B) as b:
                    for z in range(2 * K):
                        copy_z(b, z, z // K, z % K, z % 2, 0)
                    copy_s(b, 0, 0)
                    with act.Fori(0, NT // 2 - 1) as i:
                        pair(b, i, False)
                    pair(b, NT // 2 - 1, True)
                act.wait_ge(y_ok, B * NT + CREDIT)
                act.sem_inc(y_done, 1)
            with act.Else():
                with act.Fori(0, B) as b:
                    with act.Fori(0, TAPS) as k:
                        it = b * TAPS + k
                        for j in range(NT):
                            act.wait_ge(z_mm, it * NT + j + 1 + CREDIT)
                            act.wait_ge(o_mm, it * NT + CREDIT)
                            a.activation(zany[:, j * P:(j + 1) * P], Z_PS[j % 2][:, 0:P], ACT.Copy).then_inc(z_ok, 1)
                        with act.Fori(0, NT) as pt:
                            for half in range(2):
                                act.wait_ge(s_t, (it * NT + pt) * 2 + half + 1 + CREDIT)
                                act.wait_ge(o_mm, it * NT + pt + CREDIT)
                                a.activation(sq[:, half, :, 0:2 * P], S_PS[half][:, 0, :].rearrange("p (a n) -> p a n", a=2),
                                             ACT.Copy).then_inc(s_ok, 1)
                act.wait_ge(y_ok, TAPS * B * NT + CREDIT)
                act.sem_inc(y_done, 1)

            root(GN8)
            act.wait_ge(gn_ok, GN8 + 1)
            for b in range(B):
                a.activation(ysb[:, b, :], ysb[:, b, :], ACT.Identity, bias=shift_of(GN8, b),
                             scale=scale_of(GN8, b)).then_inc(y_norm, 1)
            root(GN1)
            heads(GN1, B)
            root(BN1)
            act.wait_ge(gn_ok, BN1 + 1)
            for n in range(2 * B):
                a.activation(r1[:, n // 2, (n % 2) * BIG:(n % 2 + 1) * BIG], PS[:, n, :], ACT.Relu,
                             bias=shift_of(BN1, 0), scale=scale_of(BN1, 0)).then_inc(r1_ok, 1)
            root(BN2)
            for n in range(2 * B):
                act.wait_ge(f_sum, n + 1)
                v = ysb[:, n // 2, (n % 2) * BIG:(n % 2 + 1) * BIG]
                a.activation(v, v, ACT.Relu, bias=shift_of(BN2, 0)).then_inc(f_relu, 1)

        @block.vector
        def _(dve):
            d = nc.vector
            steps = [0]

            def link(ins):
                steps[0] += 1
                ins.then_inc(dch, 1)
                dve.wait_ge(dch, steps[0])

            d.memset(woffT[:, :, :].bitcast(F32), 0.0).then_inc(pads, 1)
            d.memset(xlo[:, :, :].bitcast(F32), 0.0).then_inc(pads, 1)

            def normalise(n, grouped, weight, shift):
                nb = B if grouped is not None else 1
                mean, var = mv[:, n, 0:nb, 0], mv[:, n, 0:nb, 1]
                s = [nsm[:, n, i, 0:nb] for i in range(10)]
                if grouped is not None:
                    order, m_ps, v_ps = grouped
                    dve.wait_ge(gn_mean, order + 1)
                    link(d.tensor_copy(s[4], m_ps))
                    link(d.tensor_tensor(s[0], mean, s[4], ALU.subtract))
                    link(d.tensor_tensor(s[0], s[0], s[0], ALU.mult))
                    d.tensor_tensor(s[1], s[0], var, ALU.add).then_inc(gn_dev, 1)
                    dve.wait_ge(gn_msq, order + 1)
                    mean, var = s[4], v_ps
                d.tensor_scalar(s[2], var, EPS, None, ALU.add).then_inc(gn_var, 1)
                dve.wait_ge(gn_var, n + 1)
                dve.wait_ge(gn_std, n + 1)
                link(d.reciprocal(s[5], s[3]))
                link(d.tensor_tensor(s[6], s[5], s[5], ALU.mult))
                link(d.tensor_tensor(s[6], s[6], s[2], ALU.mult))
                link(d.tensor_scalar(s[6], s[6], -0.5, 1.5, ALU.mult, ALU.add))
                if weight is None:
                    link(d.tensor_tensor(s[8], s[5], s[6], ALU.mult))
                else:
                    link(d.scalar_tensor_tensor(out=s[8], in0=s[5], scalar=weight, in1=s[6], op0=ALU.mult, op1=ALU.mult))
                link(d.tensor_tensor(s[7], mean, s[8], ALU.mult))
                d.tensor_scalar(s[9], s[7], -1.0, shift if shift is not None else 0.0, ALU.mult, ALU.add).then_inc(gn_ok, 1)
                dve.wait_ge(gn_ok, n + 1)

            def image_stats(n, src, ready):
                for b in range(B):
                    if ready is not None:
                        ready(b)
                    for h in range(2):
                        ins = d.bn_stats(st[:, n, 2 * b + h, :], src[:, b, h * BIG:(h + 1) * BIG])
                    link(ins)
                for b in range(B):
                    ins = d.bn_aggr(mv[:, n, b, :], st[:, n, 2 * b:2 * b + 2, :])
                ins.then_inc(gn_in, 1)
                dve.wait_ge(gn_in, (GN0, GN8, GN1).index(n) + 1)

            def tails(n, count):
                for b in range(B):
                    link(d.tensor_scalar(ysb[:, b, :], xs[:, b, :], scale_of(n, b), shift_of(n, b), ALU.mult, ALU.add))
                    dve.wait_ge(xhi_ok, count + b + 1)
                    d.tensor_tensor(inner(xlo, b), square(ysb[:, b, :]), inner(xhi, b), ALU.subtract).then_inc(xlo_ok, 1)

            dve.wait_ge(woff_hi, 1)
            dve.wait_ge(pads, 3)
            d.tensor_tensor(woffT[:, :, TAIL:TAIL + OFFC], PS[:, 0, 0:TAPS * OFFC].rearrange("p (k o) -> p k o", k=TAPS),
                            woffT[:, :, 0:OFFC], ALU.subtract).then_inc(woff_ok, 1)
            image_stats(GN0, xs, lambda b: dve.wait_ge(x_in[b], 16))
            normalise(GN0, (0, O_PS[0][:, 0:B], O_PS[1][:, 0:B]), None, None)
            tails(GN0, 0)
            for m in range(K):
                dve.wait_ge(wd_hi, m + 1)
                d.tensor_tensor(wdlo[:, K * m:K * m + K, :], PS[:, 1 + m, 0:K * P].rearrange("p (k o) -> p k o", k=K),
                                wdhi[:, K * m:K * m + K, :], ALU.subtract).then_inc(wd_ok, 1)

            for i, arrived in enumerate((w1_in, w2_in)):
                dve.wait_ge(arrived, 16)
                d.tensor_reduce(tw[:, i, 0:1], wraw[i], AX.X, ALU.add)
                d.tensor_reduce(tw[:, i, 1:2], wraw[i], AX.X, ALU.max)
                link(d.tensor_reduce(tw[:, i, 3:4], wraw[i], AX.X, ALU.min))
                d.tensor_scalar(tw[:, i, 2:3], tw[:, i, 3:4], -1.0, None, ALU.mult).then_inc(tern_in, 1)
            for i in range(2):
                w, t_ = wraw[i], [tw[:, i, c:c + 1] for c in range(16)]
                dve.wait_ge(tern_red, 2 * i + 2)
                link(d.tensor_scalar(t_[7], t_[4], 1.0 / (C * C * TAPS), None, ALU.mult))
                link(d.tensor_tensor(t_[8], t_[5], t_[7], ALU.subtract))
                link(d.tensor_scalar(t_[9], t_[6], -1.0, t_[7], ALU.mult, ALU.subtract))
                link(d.tensor_tensor(t_[10], t_[8], t_[9], ALU.subtract))
                link(d.tensor_scalar(t_[10], t_[10], 1.0 / 3.0, None, ALU.mult))
                link(d.tensor_tensor(t_[11], t_[9], t_[10], ALU.add))
                link(d.tensor_tensor(t_[12], t_[8], t_[10], ALU.subtract))
                link(d.tensor_scalar(w, w, t_[7], None, ALU.subtract))
                link(d.tensor_scalar(tscr, w, t_[11], None, ALU.is_lt))
                d.scalar_tensor_tensor(out=w, in0=w, scalar=t_[12], in1=tscr, op0=ALU.is_gt,
                                       op1=ALU.subtract).then_inc(tern_ok, 1)
                dve.wait_ge(tern_ok, i + 1)

            dve.wait_ge(consts, 5 + B)
            d.tensor_scalar(ci[:, 1:2], ci[:, 0:1], 5, None, ALU.logical_shift_right)
            link(d.tensor_scalar(ci[:, 2:3], ci[:, 0:1], W - 1, None, ALU.bitwise_and))
            d.tensor_copy(byf[:, :, :], byi[:, :, :])
            d.tensor_copy(bxf[:, :], bxi[:, :])
            link(d.tensor_copy(cf[:, 0:3], ci[:, 0:3]))
            link(d.tensor_scalar(cf[:, 3:4], cf[:, 1:2], float(-W), None, ALU.mult))
            d.tensor_scalar(bxf[:, :], bxf[:, :], cf[:, 3:4], None, ALU.add)
            link(d.tensor_scalar(byf[:, :, :], byf[:, :, :], cf[:, 1:2], None, ALU.add))
            dve.wait_ge(boff_in, 16)
            dve.wait_ge(off_ok, 2 * B)
            link(d.tensor_tensor(om[:, :, :], om2[:, :, 0:OFFC], om2[:, :, TAIL:TAIL + OFFC], ALU.add))
            d.tensor_tensor(om[:, :, :], om[:, :, :], boffb[:, :].unsqueeze(1).to_broadcast([P, B * NT, OFFC]),
                            ALU.add).then_inc(om_ok, 1)
            dve.wait_ge(om_ok, 1)
            d.tensor_reduce(far[:, 0:1], om[:, :, 0:2 * TAPS], AX.XY, ALU.max, apply_absolute_value=True).then_inc(far_in, 1)
            d.tensor_tensor(py[:, :, :], om[:, :, 0:TAPS], byf[:, :, :], ALU.add)
            link(d.tensor_tensor(px[:, :, :], om[:, :, TAPS:2 * TAPS], bxf[:, :].unsqueeze(1).to_broadcast([P, B * NT, TAPS]),
                                 ALU.add))
            for c in range(W):
                ins = d.tensor_scalar(colw[:, :, :, c], px[:, :, :], float(c), None, ALU.subtract)
                if c % GRP == GRP - 1:
                    ins.then_inc(dist_ok, 1)
            dve.wait_ge(far_red, 1)
            d.tensor_scalar(fari[0:1, 0:1], far[0:1, 1:2], float(REACH), None, ALU.is_le).then_inc(far_ok, 1)
            for n in range(W // GRP):
                dve.wait_ge(abs_ok, n + 1)
                v = colw[:, :, :, n * GRP:(n + 1) * GRP]
                ins = d.tensor_scalar(v, v, 1.0, -1.0, ALU.min, ALU.add)
            link(ins)
            link(d.tensor_scalar(byf[:, :, :], byf[:, :, :], cf[:, 1:2], float(REACH), ALU.subtract, ALU.subtract))
            link(d.tensor_tensor(pyr[:, :, :], py[:, :, :], byf[:, :, :], ALU.subtract))
            dve.wait_ge(q_t, 2 * K)
            for r in range(WIN):
                ins = d.tensor_scalar(roww[:, :, :, r], pyr[:, :, :], float(r), None, ALU.subtract)
            ins.then_inc(dist_ok, 1)
            dve.wait_ge(abs_ok, W // GRP + 1)
            link(d.tensor_scalar(rowf, rowf, 1.0, -1.0, ALU.min, ALU.add))
            dve.wait_ge(mask_ok, 1)
            link(d.tensor_tensor(roww[:, :, :, :], roww[:, :, :, :],
                                 mask[:, :, :].unsqueeze(3).to_broadcast([P, B * NT, TAPS, WIN]), ALU.mult))

            dve.sem_inc(sT_ok, CREDIT)
            dve.wait_ge(far_ok, 1)
            near = dve.value_load(fari[0:1, 0:1], min_val=0, max_val=1)
            with dve.If(near == 1):
                def outer(b, i, u):
                    dve.wait_ge(s_t, b * SLOTS + 6 * i + u - 1 + CREDIT)
                    tile, ky = b * NT + 2 * i + u // K, u % K
                    rows = roww[:, bass.ds(tile, 1), K * ky:K * ky + K, :].rearrange("p t k r -> p (t k) r")
                    cols = colw[:, bass.ds(tile, 1), K * ky:K * ky + K, :].rearrange("p t k w -> p (t k) w")
                    d.tensor_tensor(sT[:, u % 2, :, :].rearrange("p k (r w) -> p k r w", w=W),
                                    rows.unsqueeze(3).to_broadcast([P, K, WIN, W]),
                                    cols.unsqueeze(2).to_broadcast([P, K, WIN, W]), ALU.mult).then_inc(sT_ok, 1)

                with dve.Fori(0, B) as b:
                    with dve.Fori(0, NT // 2) as i:
                        for u in range(6):
                            outer(b, i, u)
            with dve.Else():
                dve.wait_ge(vec_in, 7 * 16)
                d.memset(ysb[:, :, :], 0.0).then_inc(any_ok, 1)
                dve.wait_ge(any_ok, 1)
                d.tensor_scalar(ysb[:, :, :], ysb[:, :, :], v_bias, None, ALU.add).then_inc(any_ok, 1)
                dve.wait_ge(any_ok, 2)
                with dve.Fori(0, B) as b:
                    with dve.Fori(0, TAPS) as k:
                        it = b * TAPS + k
                        dve.wait_ge(sT_ok, it * NT * 2 + CREDIT)
                        pos = py[:, bass.ds(b * NT, NT), bass.ds(k, 1)].rearrange("p t k -> p (t k)")
                        d.tensor_copy(posany[:, 0, :], pos).then_inc(any_ok, 1)
                        dve.wait_ge(any_ok, it * 6 + 3)
                        d.tensor_scalar(posany[:, 1, :], posany[:, 0, :], -1.0, None, ALU.mult).then_inc(any_ok, 1)
                        dve.wait_ge(any_ok, it * 6 + 4)
                        for r in range(H):
                            ins = d.tensor_scalar(rowany[:, :, r], posany[:, 0, :], float(r), None, ALU.subtract)
                        ins.then_inc(any_ok, 1)
                        dve.wait_ge(any_ok, it * 6 + 5)
                        for r in range(H):
                            ins = d.scalar_tensor_tensor(out=rowany[:, :, r], in0=posany[:, 1, :], scalar=float(r),
                                                         in1=rowany[:, :, r], op0=ALU.add, op1=ALU.max)
                        ins.then_inc(any_ok, 1)
                        dve.wait_ge(any_ok, it * 6 + 6)
                        d.tensor_scalar(rowany[:, :, :], rowany[:, :, :], 1.0, -1.0, ALU.min, ALU.add).then_inc(any_ok, 1)
                        dve.wait_ge(any_ok, it * 6 + 7)
                        d.tensor_tensor(rowany[:, :, :], rowany[:, :, :],
                                        mask[:, bass.ds(b * NT, NT), bass.ds(k, 1)].to_broadcast([P, NT, H]),
                                        ALU.mult).then_inc(any_ok, 1)
                        dve.wait_ge(any_ok, it * 6 + 8)
                        for pt in range(NT):
                            for half in range(2):
                                n = (it * NT + pt) * 2 + half
                                dve.wait_ge(s_t, n - 1 + CREDIT)
                                cols = colw[:, bass.ds(b * NT + pt, 1), bass.ds(k, 1), :].rearrange("p t k w -> p (t k) w")
                                d.tensor_tensor(sT[:, half, 0:2, :].rearrange("p k (r w) -> p (k r) w", w=W),
                                                rowany[:, pt, half * 16:half * 16 + 16].unsqueeze(2).to_broadcast([P, 16, W]),
                                                cols.to_broadcast([P, 16, W]), ALU.mult).then_inc(sT_ok, 1)
                            dve.wait_ge(o_mm, it * NT + pt + 1 + CREDIT)
                            y = ysb[:, bass.ds(b, 1), pt * P:(pt + 1) * P].rearrange("p a n -> p (a n)")
                            d.tensor_tensor(y, y, O_PS[pt % 2][:, 0:P], ALU.add).then_inc(y_ok, 1)

            dve.wait_ge(y_done, 1)
            image_stats(GN8, ysb, None)
            normalise(GN8, (1, Z_PS[0][:, 0:B], Z_PS[1][:, 0:B]), v_gamma, v_beta)
            for b in range(B):
                dve.wait_ge(y_norm, b + 1)
                d.tensor_tensor(xs[:, b, 256:HW], xs[:, b, 256:HW], ysb[:, b, 256:HW], ALU.add).then_inc(x1_ok, 1)
            image_stats(GN1, xs, lambda b: dve.wait_ge(x1_ok, 2 * B))
            normalise(GN1, (2, S_PS[0][:, 0, 0:B], S_PS[1][:, 0, 0:B]), None, None)
            tails(GN1, B)

            def conv_stats(n, done):
                for m in range(2 * B):
                    dve.wait_ge(done, m + 1)
                    ins = d.bn_stats(st[:, n, m, :], PS[:, m, :])
                link(ins)
                link(d.bn_aggr(mv[:, n, 0, :], st[:, n, :, :]))

            conv_stats(BN1, c1_mm)
            normalise(BN1, None, v_g1, v_be1)
            for n in range(2 * B):
                b, h = n // 2, n % 2
                dve.wait_ge(r1_ok, n + 1)
                rows = slice(b * ROWS + TOP + h * 16, b * ROWS + TOP + h * 16 + 16)
                v = square(r1[:, b, h * BIG:(h + 1) * BIG])
                d.tensor_copy(xhi[:, rows, 1:1 + W], v).then_inc(r1hi_ok, 1)
                dve.wait_ge(r1hi_ok, n + 1)
                d.tensor_tensor(xlo[:, rows, 1:1 + W], v, xhi[:, rows, 1:1 + W], ALU.subtract).then_inc(r1lo_ok, 1)
            conv_stats(BN2, c2_mm)
            normalise(BN2, None, v_g2, v_be2)

            def finish(n):
                dve.wait_ge(f_relu, n + 1)
                v = slice((n % 2) * BIG, (n % 2 + 1) * BIG)
                d.tensor_tensor(ysb[:, n // 2, v], ysb[:, n // 2, v], xs[:, n // 2, v], ALU.add).then_inc(f_ok, 1)

            for n in range(2 * B):
                v = slice((n % 2) * BIG, (n % 2 + 1) * BIG)
                d.scalar_tensor_tensor(out=ysb[:, n // 2, v], in0=PS[:, n, :], scalar=scale_of(BN2, 0),
                                       in1=r1[:, n // 2, v], op0=ALU.mult, op1=ALU.add).then_inc(f_sum, 1)
                if n >= 2:
                    finish(n - 2)
            finish(2 * B - 2)
            finish(2 * B - 1)


_INS = ["x", "L0_conv_w_off", "L0_conv_b_off", "L0_conv_weight", "L0_conv_bias", "L0_conv_gamma", "L0_conv_beta",
        "L1_conv_w1", "L1_conv_gamma1", "L1_conv_beta1", "L1_conv_w2", "L1_conv_gamma2", "L1_conv_beta2"]


def kernel(**inputs):
    import numpy as np
    import concourse.bacc as bacc
    from concourse.bass_utils import run_bass_kernel_spmd

    nc = bacc.Bacc("TRN2", target_bir_lowering=False, num_devices=1)
    arrays, args = {}, []
    for name in _INS:
        arrays[f"in_{name}"] = a = np.ascontiguousarray(inputs[name])
        args.append(nc.dram_tensor(f"in_{name}", a.shape, mybir.dt.from_np(a.dtype), kind="ExternalInput").ap())
    out = nc.dram_tensor("out", (B, C, H, W), F32, kind="ExternalOutput").ap()
    build(nc, *args, out)
    r = run_bass_kernel_spmd(nc, [arrays], core_ids=[0])
    return r.results[0]["out"]
```

```python
from contextlib import ExitStack

import concourse.bass as bass
from concourse import mybir

F32 = mybir.dt.float32
F32R = mybir.dt.float32r
I32 = mybir.dt.int32
ALU = mybir.AluOpType
ACT = mybir.ActivationFunctionType
AX = mybir.AxisListType

B, C, H, W = 4, 128, 32, 32
P = 128
K = 3
TAPS = K * K
HW = H * W
TR = P // W
NT = HW // P
REACH = 2
WIN = 2 * TR
TOP = REACH + 1
ROWS = H + TR
PROWS = B * ROWS + 2
PW = W + 2
OFFC = 3 * TAPS
GRP = 32
NG = P // GRP
TILES = B * NT
EPS = 1e-5
SLOTS = NT * K
ZPER = (NT + 1) * K
BIG = 512


def build(nc, x, w_off, b_off, wd, bias, gamma, beta, w1, g1, be1, w2, g2, be2, out):
    x_v = x.rearrange("b c h w -> c b (h w)")
    out_v = out.rearrange("b c h w -> c b (h w)")
    flat = "o c h w -> o (c h w)"

    with ExitStack() as ctx:
        def sb(name, shape, dt=F32):
            return ctx.enter_context(nc.sbuf_tensor(name, shape, dt))

        def sem(name):
            return ctx.enter_context(nc.semaphore(name))

        xs = sb("xs", [P, B, HW])
        xhi = sb("xhi", [P, PROWS, PW], F32R)
        xlo = sb("xlo", [P, PROWS, PW], F32R)
        ysb = sb("ysb", [P, B, HW])
        r1 = sb("r1", [P, B, HW])
        hx = sb("hx", [P, 2, TAPS * TR, W])
        roww = sb("roww", [P, TILES, TAPS * TR, 2])
        woff_raw = sb("woff_raw", [OFFC, C * TAPS])
        wd_raw = sb("wd_raw", [P, C * TAPS])
        woffT = sb("woffT", [P, TAPS, P], F32R)
        wdhi = sb("wdhi", [P, TAPS, P], F32R)
        wdlo = sb("wdlo", [P, TAPS, P], F32R)
        q1 = sb("q1", [P, TAPS, P], F32R)
        q2 = sb("q2", [P, TAPS, P], F32R)
        omt = sb("omt", [GRP, 2, BIG])
        omh = sb("omh", [GRP, 2, BIG])
        omr = sb("omr", [P, B * H, GRP])
        xwin = sb("xwin", [P, 2, 2, K + TR - 1, W], F32R)
        zr = sb("zr", [P, 2, K, K, P])
        vt = sb("vt", [P, 2, K * TR, 2, W])
        sq = sb("sq", [P, 2, K * TR, 2, W])
        ident = sb("ident", [P, P])
        g32 = sb("g32", [P, P])
        g16 = sb("g16", [P, P])
        boffc = sb("boffc", [GRP, 1])
        vec = sb("vec", [P, 8])
        ci = sb("ci", [P, 4], I32)
        cf = sb("cf", [P, 4])
        bxi = sb("bxi", [P, TAPS], I32)
        bxf = sb("bxf", [P, TAPS])
        coli = sb("coli", [P, W], I32)
        colf = sb("colf", [P, W])
        rowj = sb("rowj", [P, NT])
        px = sb("px", [P, TILES, TAPS * TR])
        py = sb("py", [P, TILES, TAPS * TR])
        mask = sb("mask", [P, TILES, TAPS * TR])
        rowany = sb("rowany", [P, 2, NT * TR, NT])
        st = sb("st", [P, 5, 2 * B, 6])
        mv = sb("mv", [P, 5, B, 2])
        nsm = sb("nsm", [P, 5, 10, B])
        tw = sb("tw", [P, 2, 16])
        far = sb("far", [P, B + 2])
        fari = sb("fari", [1, 1], I32)
        r1f = r1[:, :, :].rearrange("p b n -> p (b n)")
        wraw = [r1f[:, i * C * TAPS:(i + 1) * C * TAPS] for i in range(2)]
        wscr = r1f[:, 2 * C * TAPS:3 * C * TAPS]
        zf = zr[:, :, :, :, :].rearrange("p a b c o -> p (a b c o)")
        byf, rbf = (zf[:, i * TILES * TAPS * TR:(i + 1) * TILES * TAPS * TR].rearrange("p (t n) -> p t n", t=TILES)
                    for i in range(2))
        byi, rbi = (m[:, :, :, :, :].rearrange("p a b c w -> p (a b c w)")[:, 0:TILES * TAPS * TR]
                    .rearrange("p (t n) -> p t n", t=TILES) for m in (vt, sq))
        zany = omr[:, 0:HW // GRP, :].rearrange("p h c -> p (h c)")

        PS = ctx.enter_context(nc.psum_tensor("PS", [P, 2 * B, BIG], F32))
        Z_PS = [PS[:, 4, :], PS[:, 5, :]]
        ZB_PS = [PS[:, 2, :], PS[:, 3, :]]
        O_PS = [PS[:, 6, :], PS[:, 7, :]]

        x_in = [sem(f"x_in{b}") for b in range(B)]
        woff_in, wd_in, w1_in, w2_in, vec_in, boff_in = (
            sem(n) for n in ("woff_in", "wd_in", "w1_in", "w2_in", "vec_in", "boff_in"))
        gps = sem("gps")
        consts = sem("consts")
        dch = sem("dch")
        pads = sem("pads")
        gn_in, gn_mean, gn_dev, gn_msq, gn_var, gn_std = (
            sem(n) for n in ("gn_in", "gn_mean", "gn_dev", "gn_msq", "gn_var", "gn_std"))
        gn_ok = sem("gn_ok")
        xhi_ok, xlo_ok = sem("xhi_ok"), sem("xlo_ok")
        woff_t, woff_hi, woff_ok = sem("woff_t"), sem("woff_hi"), sem("woff_ok")
        wd_t, wd_hi, wd_ok = sem("wd_t"), sem("wd_hi"), sem("wd_ok")
        off_mm, off_tail, off_sum, off_t, off_ok = (sem(n) for n in ("off_mm", "off_tail", "off_sum", "off_t", "off_ok"))
        by_i, by_f = sem("by_i"), sem("by_f")
        pos_ok, mask_ok, row_d, row_h, row_ok = (sem(n) for n in ("pos_ok", "mask_ok", "row_d", "row_h", "row_ok"))
        far_in, far_red, far_ok = sem("far_in"), sem("far_red"), sem("far_ok")
        tern_in, tern_red, tern_th, tern_s, tern_ok = (
            sem(n) for n in ("tern_in", "tern_red", "tern_th", "tern_s", "tern_ok"))
        q_t, q_ok = sem("q_t"), sem("q_ok")
        hx_d, hx_a, hx_ok = sem("hx_d"), sem("hx_a"), sem("hx_ok")
        v_ok, s_ok = sem("v_ok"), sem("s_ok")
        xw_ok, z_mm, z_ok = sem("xw_ok"), sem("z_mm"), sem("z_ok")
        o_mm, y_ok = sem("o_mm"), sem("y_ok")
        any_ok = sem("any_ok")
        y_done = sem("y_done")
        y_norm, x1_ok = sem("y_norm"), sem("x1_ok")
        c1_mm, c2_mm = sem("c1_mm"), sem("c2_mm")
        r1_ok, r1hi_ok, r1lo_ok = sem("r1_ok"), sem("r1hi_ok"), sem("r1lo_ok")
        f_sum, f_relu, f_ok, out_done = (sem(n) for n in ("f_sum", "f_relu", "f_ok", "out_done"))

        CREDIT = 2
        GN0, GN8, GN1, BN1, BN2 = range(5)
        v_bias, v_gamma, v_beta, v_g1, v_be1, v_g2, v_be2 = (vec[:, i:i + 1] for i in range(7))

        def scale_of(n, b):
            return nsm[:, n, 8, b:b + 1]

        def shift_of(n, b):
            return nsm[:, n, 9, b:b + 1]

        def inner(img, b):
            return img[:, b * ROWS + TOP:b * ROWS + TOP + H, 1:1 + W]

        def sany(m, half):
            return m[:, half, :, :, :].rearrange("p n r w -> p (n r w)")[:, 0:4 * P].rearrange("p (j n) -> p j n", j=4)

        def square(a):
            return a.rearrange("p (h w) -> p h w", w=W)

        block = ctx.enter_context(nc.Block())

        @block.sync
        def _(sp):
            for b in range(B):
                sp.dma_start(xs[:, b, :], x_v[:, b, :]).then_inc(x_in[b], 16)
            sp.dma_start(wraw[0], w1.rearrange(flat)).then_inc(w1_in, 16)
            sp.dma_start(wraw[1], w2.rearrange(flat)).then_inc(w2_in, 16)
            for i, v in enumerate((bias, gamma, beta, g1, be1, g2, be2)):
                sp.dma_start(vec[:, i:i + 1], v.rearrange("(c a) -> c a", a=1)).then_inc(vec_in, 16)
            for n in range(2 * B):
                sp.wait_ge(f_ok, n + 1)
                sp.dma_start(out_v[:, n // 2, (n % 2) * BIG:(n % 2 + 1) * BIG],
                             ysb[:, n // 2, (n % 2) * BIG:(n % 2 + 1) * BIG]).then_inc(out_done, 16)
            sp.wait_ge(out_done, 16 * 2 * B)

        @block.gpsimd
        def _(pool):
            g = nc.gpsimd
            g.memset(ident[:, :], 1.0).then_inc(gps, 1)
            g.memset(g32[:, :], 0.25).then_inc(gps, 1)
            g.memset(g16[:, :], 0.125).then_inc(gps, 1)
            pool.wait_ge(gps, 3)
            g.affine_select(out=ident[:, :], in_=ident[:, :], compare_op=ALU.is_equal, fill=0.0, base=0,
                            pattern=[[-1, P]], channel_multiplier=1).then_inc(consts, 1)
            for m, n in ((g32, 4), (g16, 8)):
                v = m[:, :].rearrange("p (g n) -> p g n", n=n)
                g.affine_select(out=v, in_=v, compare_op=ALU.is_ge, fill=0.0, base=0,
                                pattern=[[-n, P // n], [0, n]], channel_multiplier=1).then_inc(gps, 1)
            pool.wait_ge(gps, 5)
            for m, n in ((g32, 4), (g16, 8)):
                v = m[:, :].rearrange("p (g n) -> p g n", n=n)
                g.affine_select(out=v, in_=v, compare_op=ALU.is_ge, fill=0.0, base=n - 1,
                                pattern=[[n, P // n], [0, n]], channel_multiplier=-1).then_inc(consts, 1)
            g.memset(xhi[:, :, :].bitcast(F32), 0.0).then_inc(pads, 1)
            g.iota(ci[:, 0:1], [[0, 1]], base=0, channel_multiplier=1).then_inc(consts, 1)
            g.iota(bxi[:, :], [[0, K], [1, K]], base=-1, channel_multiplier=0).then_inc(consts, 1)
            g.iota(coli[:, :], [[1, W]], base=0, channel_multiplier=0).then_inc(consts, 1)
            for b in range(B):
                for m, top, row in ((byi, -1, 1), (rbi, -TOP, 0)):
                    g.iota(m[:, b * NT:(b + 1) * NT, :].bitcast(I32), [[TR, NT], [1, K], [0, K], [row, TR]], base=top,
                           channel_multiplier=0).then_inc(by_i, 1)
            for i in range(2):
                pool.wait_ge(tern_in, i + 1)
                g.partition_all_reduce(tw[:, i, 4:5], tw[:, i, 0:1], P, bass.bass_isa.ReduceOp.add).then_inc(tern_red, 1)
                g.partition_all_reduce(tw[:, i, 5:7], tw[:, i, 1:3], P, bass.bass_isa.ReduceOp.max).then_inc(tern_red, 1)
            for i in range(2):
                pool.wait_ge(tern_th, i + 1)
                g.tensor_scalar(wraw[i], wraw[i], tw[:, i, 7:8], None, ALU.subtract).then_inc(tern_s, 1)
                pool.wait_ge(tern_s, 3 * i + 1)
                g.tensor_scalar(wscr, wraw[i], tw[:, i, 11:12], None, ALU.is_lt).then_inc(tern_s, 1)
                pool.wait_ge(tern_s, 3 * i + 2)
                g.tensor_scalar(wraw[i], wraw[i], tw[:, i, 12:13], None, ALU.is_gt).then_inc(tern_s, 1)
                pool.wait_ge(tern_s, 3 * i + 3)
                g.tensor_tensor(wraw[i], wraw[i], wscr, ALU.subtract).then_inc(tern_ok, 1)
                pool.wait_ge(tern_ok, i + 1)
            pool.wait_ge(far_in, 1)
            g.partition_all_reduce(far[:, B + 1:B + 2], far[:, B:B + 1], P, bass.bass_isa.ReduceOp.max).then_inc(far_red, 1)

            pool.sem_inc(v_ok, CREDIT)
            pool.wait_ge(far_ok, 1)
            near = pool.value_load(fari[0:1, 0:1], min_val=0, max_val=1)
            with pool.If(near == 1):
                def outer(b, i, u):
                    tile, ky, par = b * NT + 2 * i + u // K, u % K, u // K
                    if ky == 0:
                        pool.wait_ge(hx_ok, tile + 1)
                    pool.wait_ge(s_ok, b * SLOTS + 6 * i + u - 1 + CREDIT)
                    n = K * TR
                    rows = roww[:, bass.ds(tile, 1), n * ky:n * ky + n, :].rearrange("p t n r -> p (t n) r")
                    g.tensor_tensor(vt[:, u % 2, :, :, :], rows.unsqueeze(3).to_broadcast([P, n, 2, W]),
                                    hx[:, par, n * ky:n * ky + n, :].unsqueeze(2).to_broadcast([P, n, 2, W]),
                                    ALU.mult).then_inc(v_ok, 1)

                for b in range(B):
                    with pool.Fori(0, NT // 2) as i:
                        for u in range(6):
                            outer(b, i, u)

            for b in range(B):
                pool.wait_ge(y_norm, b + 1)
                g.tensor_tensor(xs[:, b, 0:256], xs[:, b, 0:256], ysb[:, b, 0:256], ALU.add).then_inc(x1_ok, 1)

        @block.tensor
        def _(pe):
            t = nc.tensor
            pe.wait_ge(consts, 3)
            pe.wait_ge(woff_in, 16)
            v = woff_raw[:, :].rearrange("o (c k) -> o k c", k=TAPS)
            for k in range(TAPS):
                last = t.transpose(PS[:, 0, k * OFFC:(k + 1) * OFFC], v[:, k, :], ident[0:OFFC, 0:OFFC])
            last.then_inc(woff_t, 1)
            pe.wait_ge(wd_in, 16)
            v = wd_raw[:, :].rearrange("o (c k) -> o k c", k=TAPS)
            for k in range(TAPS):
                last = t.transpose(PS[:, 1 + k // K, (k % K) * P:(k % K + 1) * P], v[:, k, :], ident[:, :])
                if k % K == K - 1:
                    last.then_inc(wd_t, 1)

            def group_sums(n, mat, m_ps, v_ps):
                pe.wait_ge(gn_in, n + 1)
                t.matmul(m_ps, mat[:, :], mv[:, (GN0, GN8, GN1)[n], :, 0], start=True, stop=True).then_inc(gn_mean, 1)
                pe.wait_ge(gn_dev, n + 1)
                t.matmul(v_ps, mat[:, :], nsm[:, (GN0, GN8, GN1)[n], 1, :], start=True, stop=True).then_inc(gn_msq, 1)

            group_sums(0, g32, O_PS[0][:, 0:B], O_PS[1][:, 0:B])

            pe.wait_ge(woff_ok, 1)
            for b in range(B):
                pe.wait_ge(xhi_ok, b + 1)
                pe.wait_ge(xlo_ok, b + 1)
                for h in range(2):
                    if b:
                        pe.wait_ge(off_sum, 2 * b + h - 1)
                    for k in range(TAPS):
                        r = b * ROWS + TOP - 1 + h * (H // 2) + k // K
                        for part, src in enumerate((xhi, xlo)):
                            last = t.matmul(Z_PS[h], woffT[:, k, :], src[:, r:r + H // 2, k % K:k % K + W],
                                            start=(k == 0 and part == 0), stop=(k == TAPS - 1 and part == 1))
                    last.then_inc(off_mm, 1)

            pe.wait_ge(wd_hi, K)
            pe.wait_ge(wd_ok, K)
            for i in range(2):
                pe.wait_ge(tern_ok, i + 1)
                v = wraw[i].rearrange("o (c k) -> o k c", k=TAPS)
                for m in range(K):
                    if i:
                        pe.wait_ge(q_ok, m + 1)
                    for k in range(K * m, K * m + K):
                        last = t.transpose(PS[:, 1 + m, (k % K) * P:(k % K + 1) * P], v[:, k, :], ident[:, :])
                    last.then_inc(q_t, 1)
            pe.wait_ge(q_ok, 2 * K)
            pe.wait_ge(off_sum, 2 * B)

            for s in (z_mm, o_mm):
                pe.sem_inc(s, CREDIT)

            def z_block(bank, par, ky, w_taps):
                n = w_taps(wdhi)
                win = [xwin[:, part, par, ky:ky + TR, :].rearrange("p r w -> p (r w)") for part in range(2)]
                dst = bank[:, 0:n.shape[-1]]
                t.matmul(dst, win[0], n, start=True, stop=False)
                t.matmul(dst, win[1], n, start=False, stop=False)
                t.matmul(dst, win[0], w_taps(wdlo), start=False, stop=True).then_inc(z_mm, 1)

            pe.wait_ge(far_ok, 1)
            near = pe.value_load(fari[0:1, 0:1], min_val=0, max_val=1)
            with pe.If(near == 1):
                def multiply(b, s, par, ky, spar, pt, z):
                    pe.wait_ge(s_ok, b * SLOTS + s + 1 + CREDIT)
                    pe.wait_ge(z_ok, b * ZPER + z + CREDIT)
                    if ky == 0:
                        pe.wait_ge(y_ok, b * NT + pt - 1 + CREDIT)
                    for kx in range(K):
                        for blk in range(2):
                            last = t.matmul(O_PS[par][:, 0:P], zr[:, (par + blk) % 2, ky, kx, :],
                                            sq[:, spar, TR * kx:TR * kx + TR, blk, :],
                                            start=(ky == 0 and kx == 0 and blk == 0),
                                            stop=(ky == K - 1 and kx == K - 1 and blk == 1))
                    last.then_inc(o_mm, 1)

                def taps_of(ky):
                    return lambda w: w[:, K * ky:K * ky + K, :].rearrange("p k o -> p (k o)")

                def seam(b, ky):
                    if ky == 0:
                        pe.wait_ge(xw_ok, (b * (NT + 1) + 2) * 2)
                    if b or ky == K - 1:
                        pe.wait_ge(z_ok, b * ZPER - 1 + ky + CREDIT)
                    z_block(Z_PS[(ky + 1) % 2], 0, ky, taps_of(ky))
                    if ky == K - 1:
                        pe.wait_ge(z_ok, b * ZPER + 2 + CREDIT)
                    z_block(ZB_PS[ky % 2], 1, ky, taps_of(ky))

                def pair(b, i, first=False, final=False):
                    for par in range(2):
                        for ky in range(K):
                            u = K * par + ky
                            pt, z = 2 * i + par, 6 * i + u + 6
                            if not (final and par == 1):
                                if ky == 0:
                                    pe.wait_ge(xw_ok, (b * (NT + 1) + pt + 3) * 2)
                                pe.wait_ge(z_ok, b * ZPER + (z - 1 if not first or u > 1 else (3, 5)[u]) + CREDIT)
                                z_block(Z_PS[u % 2], par, ky, taps_of(ky))
                            elif b < B - 1:
                                seam(b + 1, ky)
                            multiply(b, 6 * i + u, par, ky, u % 2, pt, 2 * ky + 2 if first and par == 0 else z - 2)

                for ky in range(K):
                    seam(0, ky)
                for b in range(B):
                    pair(b, 0, first=True)
                    with pe.Fori(1, NT // 2 - 1) as i:
                        pair(b, i)
                    pair(b, NT // 2 - 1, final=True)
            with pe.Else():
                with pe.Fori(0, B) as b:
                    with pe.Fori(0, TAPS) as k:
                        it = b * TAPS + k
                        for j in range(NT):
                            pe.wait_ge(xw_ok, (it * NT + j + 1) * 2)
                            pe.wait_ge(z_ok, it * NT + j - 1 + CREDIT)
                            z_block(Z_PS[j % 2], j % 2, 0, lambda w: w[:, bass.ds(k, 1), :].rearrange("p k o -> p (k o)"))
                        with pe.Fori(0, NT // 2) as i:
                            for par in range(2):
                                pe.wait_ge(z_ok, (it + 1) * NT + CREDIT)
                                pe.wait_ge(y_ok, it * NT + 2 * i + par - 1 + CREDIT)
                                for j in range(NT):
                                    if j % 4 == 0:
                                        pe.wait_ge(s_ok, (it * NT + 2 * i + par) * 2 + j // 4 + 1 + CREDIT)
                                    last = t.matmul(O_PS[par][:, 0:P], zany[:, j * P:(j + 1) * P], sany(sq, j // 4)[:, j % 4, :],
                                                    start=(j == 0), stop=(j == NT - 1))
                                last.then_inc(o_mm, 1)

            group_sums(1, g16, Z_PS[0][:, 0:B], Z_PS[1][:, 0:B])
            group_sums(2, g32, O_PS[0][:, 0:B], O_PS[1][:, 0:B])
            pe.wait_ge(gn_ok, 3)

            def conv(q, b, done):
                for h in range(2):
                    for k in range(TAPS):
                        r = b * ROWS + TOP - 1 + h * (H // 2) + k // K
                        for part, src in enumerate((xhi, xlo)):
                            last = t.matmul(PS[:, bass.ds(2 * b + h, 1), :].rearrange("p a n -> p (a n)"), q[:, k, :],
                                            src[:, bass.ds(r, H // 2), k % K:k % K + W],
                                            start=(k == 0 and part == 0), stop=(k == TAPS - 1 and part == 1))
                    last.then_inc(done, 1)

            with pe.Fori(0, B) as b:
                pe.wait_ge(xhi_ok, B + b + 1)
                pe.wait_ge(xlo_ok, B + b + 1)
                conv(q1, b, c1_mm)
            with pe.Fori(0, B) as b:
                pe.wait_ge(r1hi_ok, 2 * b + 2)
                pe.wait_ge(r1lo_ok, 2 * b + 2)
                conv(q2, b, c2_mm)

        @block.scalar
        def _(act):
            a = nc.scalar
            act.dma_start(woff_raw[:, :], w_off.rearrange(flat)).then_inc(woff_in, 16)
            act.dma_start(wd_raw[:, :], wd.rearrange(flat)).then_inc(wd_in, 16)
            act.wait_ge(pads, 4)
            act.dma_start(boffc[0:OFFC, :], b_off.rearrange("(c a) -> c a", a=1)).then_inc(boff_in, 16)
            act.wait_ge(woff_t, 1)
            a.activation(woffT[:, :, 0:OFFC], PS[:, 0, 0:TAPS * OFFC].rearrange("p (k o) -> p k o", k=TAPS),
                         ACT.Copy).then_inc(woff_hi, 1)

            def root(n):
                act.wait_ge(gn_var, n + 1)
                nb = 1 if n in (BN1, BN2) else B
                a.activation(nsm[:, n, 3, 0:nb], nsm[:, n, 2, 0:nb], ACT.Sqrt).then_inc(gn_std, 1)

            def heads(n, count):
                act.wait_ge(gn_ok, n + 1)
                for b in range(B):
                    a.activation(inner(xhi, b), square(xs[:, b, :]), ACT.Identity, bias=shift_of(n, b),
                                 scale=scale_of(n, b)).then_inc(xhi_ok, 1)

            root(GN0)
            heads(GN0, 0)
            for m in range(K):
                act.wait_ge(wd_t, m + 1)
                a.activation(wdhi[:, K * m:K * m + K, :], PS[:, 1 + m, 0:K * P].rearrange("p (k o) -> p k o", k=K),
                             ACT.Copy).then_inc(wd_hi, 1)
            def regroup(n):
                act.wait_ge(off_t, n + 1)
                rows = slice(n * H // 2, (n + 1) * H // 2)
                for g in range(2):
                    a.activation(omr[(g + 2) * GRP:(g + 3) * GRP, rows, :], omr[g * GRP:(g + 1) * GRP, rows, :],
                                 ACT.Copy).then_inc(off_ok, 1)

            def row_profiles(b):
                tiles = slice(b * NT, (b + 1) * NT)
                act.wait_ge(off_ok, 4 * b + 4)
                logits = omr[:, b * H:(b + 1) * H, 2 * TAPS:OFFC].rearrange("p (t a) k -> p t k a", a=TR)
                a.activation(mask[:, tiles, :].rearrange("p t (k a) -> p t k a", a=TR), logits, ACT.Sigmoid).then_inc(mask_ok, 1)
                act.wait_ge(row_d, b + 1)
                v = roww[:, tiles, :, :]
                a.activation(v, v, ACT.Abs).then_inc(row_h, 1)
                act.wait_ge(row_h, 2 * b + 1)
                a.activation(v, v, ACT.Relu, scale=-1.0, bias=1.0).then_inc(row_h, 1)

            for n in range(2 * B):
                act.wait_ge(off_mm, n + 1)
                if n >= 2:
                    act.wait_ge(off_sum, n - 1)
                a.activation(omt[:, n % 2, :], Z_PS[n % 2][GRP:2 * GRP, :], ACT.Copy).then_inc(off_tail, 1)
                if n >= 1:
                    regroup(n - 1)
                if n >= 3 and n % 2:
                    row_profiles(n // 2 - 1)
            regroup(2 * B - 1)
            row_profiles(B - 1)
            for i, q in enumerate((q1, q2)):
                for m in range(K):
                    act.wait_ge(q_t, K * i + m + 1)
                    a.activation(q[:, K * m:K * m + K, :], PS[:, 1 + m, 0:K * P].rearrange("p (k o) -> p k o", k=K),
                                 ACT.Copy).then_inc(q_ok, 1)

            for s in (z_ok, y_ok):
                act.sem_inc(s, CREDIT)
            act.wait_ge(vec_in, 7 * 16)
            act.wait_ge(far_ok, 1)
            near = act.value_load(fari[0:1, 0:1], min_val=0, max_val=1)
            with act.If(near == 1):
                def hats(tile, par):
                    act.wait_ge(hx_d, tile + 1)
                    a.activation(hx[:, par, :, :], hx[:, par, :, :], ACT.Abs).then_inc(hx_a, 1)
                    act.wait_ge(hx_a, tile + 1)
                    a.activation(hx[:, par, :, :], hx[:, par, :, :], ACT.Relu, scale=-1.0, bias=1.0).then_inc(hx_ok, 1)

                def copy_z(b, z, par, ky, bank, used):
                    act.wait_ge(z_mm, b * ZPER + z + 1 + CREDIT)
                    act.wait_ge(o_mm, used + CREDIT)
                    a.activation(zr[:, par, ky, :, :], bank[:, 0:K * P].rearrange("p (k o) -> p k o", k=K),
                                 ACT.Copy).then_inc(z_ok, 1)

                def seam(b, ky):
                    for j, bank in enumerate((Z_PS[(ky + 1) % 2], ZB_PS[ky % 2])):
                        copy_z(b, 2 * ky + j, j, ky, bank, b * SLOTS - K + ky + 1 if b else 0)

                def pair(b, i, final):
                    for par in range(2):
                        for ky in range(K):
                            u = K * par + ky
                            if not (final and par == 1):
                                copy_z(b, 6 * i + u + 6, par, ky, Z_PS[u % 2], b * SLOTS + 6 * i + u + 1)
                            elif b < B - 1:
                                seam(b + 1, ky)
                        act.wait_ge(o_mm, b * SLOTS + 6 * i + K * par + K + CREDIT)
                        a.activation(ysb[:, b, bass.ds((2 * i + par) * P, P)], O_PS[par][:, 0:P], ACT.Identity,
                                     bias=v_bias).then_inc(y_ok, 1)
                        if not (final and b == B - 1):
                            hats(b * NT + 2 * i + par + 2, par)

                for par in range(2):
                    hats(par, par)
                for ky in range(K):
                    seam(0, ky)
                for b in range(B):
                    with act.Fori(0, NT // 2 - 1) as i:
                        pair(b, i, False)
                    pair(b, NT // 2 - 1, True)
                act.wait_ge(y_ok, B * NT + CREDIT)
                act.sem_inc(y_done, 1)
            with act.Else():
                with act.Fori(0, B) as b:
                    with act.Fori(0, TAPS) as k:
                        it = b * TAPS + k
                        for j in range(NT):
                            act.wait_ge(z_mm, it * NT + j + 1 + CREDIT)
                            act.wait_ge(o_mm, it * NT + CREDIT)
                            a.activation(zany[:, j * P:(j + 1) * P], Z_PS[j % 2][:, 0:P], ACT.Copy).then_inc(z_ok, 1)
                act.wait_ge(y_ok, TAPS * B * NT + CREDIT)
                act.sem_inc(y_done, 1)

            root(GN8)
            act.wait_ge(gn_ok, GN8 + 1)
            for b in range(B):
                a.activation(ysb[:, b, :], ysb[:, b, :], ACT.Identity, bias=shift_of(GN8, b),
                             scale=scale_of(GN8, b)).then_inc(y_norm, 1)
            root(GN1)
            heads(GN1, B)
            root(BN1)
            act.wait_ge(gn_ok, BN1 + 1)
            for n in range(2 * B):
                a.activation(r1[:, n // 2, (n % 2) * BIG:(n % 2 + 1) * BIG], PS[:, n, :], ACT.Relu,
                             bias=shift_of(BN1, 0), scale=scale_of(BN1, 0)).then_inc(r1_ok, 1)
            root(BN2)
            for n in range(2 * B):
                act.wait_ge(f_sum, n + 1)
                v = ysb[:, n // 2, (n % 2) * BIG:(n % 2 + 1) * BIG]
                a.activation(v, v, ACT.Relu, bias=shift_of(BN2, 0)).then_inc(f_relu, 1)

        @block.vector
        def _(dve):
            d = nc.vector
            steps = [0]

            def link(ins):
                steps[0] += 1
                ins.then_inc(dch, 1)
                dve.wait_ge(dch, steps[0])

            d.memset(woffT[:, :, :].bitcast(F32), 0.0).then_inc(pads, 1)
            d.memset(boffc[:, :], 0.0).then_inc(pads, 1)
            d.memset(xlo[:, :, :].bitcast(F32), 0.0).then_inc(pads, 1)

            def normalise(n, grouped, weight, shift):
                nb = B if grouped is not None else 1
                mean, var = mv[:, n, 0:nb, 0], mv[:, n, 0:nb, 1]
                s = [nsm[:, n, i, 0:nb] for i in range(10)]
                if grouped is not None:
                    order, m_ps, v_ps = grouped
                    dve.wait_ge(gn_mean, order + 1)
                    link(d.tensor_copy(s[4], m_ps))
                    link(d.tensor_tensor(s[0], mean, s[4], ALU.subtract))
                    link(d.tensor_tensor(s[0], s[0], s[0], ALU.mult))
                    d.tensor_tensor(s[1], s[0], var, ALU.add).then_inc(gn_dev, 1)
                    dve.wait_ge(gn_msq, order + 1)
                    mean, var = s[4], v_ps
                d.tensor_scalar(s[2], var, EPS, None, ALU.add).then_inc(gn_var, 1)
                dve.wait_ge(gn_var, n + 1)
                dve.wait_ge(gn_std, n + 1)
                link(d.reciprocal(s[5], s[3]))
                link(d.tensor_tensor(s[6], s[5], s[5], ALU.mult))
                link(d.tensor_tensor(s[6], s[6], s[2], ALU.mult))
                link(d.tensor_scalar(s[6], s[6], -0.5, 1.5, ALU.mult, ALU.add))
                if weight is None:
                    link(d.tensor_tensor(s[8], s[5], s[6], ALU.mult))
                else:
                    link(d.scalar_tensor_tensor(out=s[8], in0=s[5], scalar=weight, in1=s[6], op0=ALU.mult, op1=ALU.mult))
                link(d.tensor_tensor(s[7], mean, s[8], ALU.mult))
                d.tensor_scalar(s[9], s[7], -1.0, shift if shift is not None else 0.0, ALU.mult, ALU.add).then_inc(gn_ok, 1)
                dve.wait_ge(gn_ok, n + 1)

            def image_stats(n, src, ready):
                for b in range(B):
                    if ready is not None:
                        ready(b)
                    for h in range(2):
                        ins = d.bn_stats(st[:, n, 2 * b + h, :], src[:, b, h * BIG:(h + 1) * BIG])
                    link(ins)
                for b in range(B):
                    ins = d.bn_aggr(mv[:, n, b, :], st[:, n, 2 * b:2 * b + 2, :])
                ins.then_inc(gn_in, 1)
                dve.wait_ge(gn_in, (GN0, GN8, GN1).index(n) + 1)

            def tails(n, count):
                for b in range(B):
                    link(d.tensor_scalar(ysb[:, b, :], xs[:, b, :], scale_of(n, b), shift_of(n, b), ALU.mult, ALU.add))
                    dve.wait_ge(xhi_ok, count + b + 1)
                    d.tensor_tensor(inner(xlo, b), square(ysb[:, b, :]), inner(xhi, b), ALU.subtract).then_inc(xlo_ok, 1)

            dve.wait_ge(woff_hi, 1)
            dve.wait_ge(pads, 4)
            d.tensor_tensor(woffT[:, :, GRP:GRP + OFFC], PS[:, 0, 0:TAPS * OFFC].rearrange("p (k o) -> p k o", k=TAPS),
                            woffT[:, :, 0:OFFC], ALU.subtract).then_inc(woff_ok, 1)
            image_stats(GN0, xs, lambda b: dve.wait_ge(x_in[b], 16))
            normalise(GN0, (0, O_PS[0][:, 0:B], O_PS[1][:, 0:B]), None, None)
            tails(GN0, 0)
            for m in range(K):
                dve.wait_ge(wd_hi, m + 1)
                d.tensor_tensor(wdlo[:, K * m:K * m + K, :], PS[:, 1 + m, 0:K * P].rearrange("p (k o) -> p k o", k=K),
                                wdhi[:, K * m:K * m + K, :], ALU.subtract).then_inc(wd_ok, 1)

            for i, arrived in enumerate((w1_in, w2_in)):
                dve.wait_ge(arrived, 16)
                d.tensor_reduce(tw[:, i, 0:1], wraw[i], AX.X, ALU.add)
                d.tensor_reduce(tw[:, i, 1:2], wraw[i], AX.X, ALU.max)
                link(d.tensor_reduce(tw[:, i, 3:4], wraw[i], AX.X, ALU.min))
                d.tensor_scalar(tw[:, i, 2:3], tw[:, i, 3:4], -1.0, None, ALU.mult).then_inc(tern_in, 1)
            def thresholds(i):
                t_ = [tw[:, i, c:c + 1] for c in range(16)]
                dve.wait_ge(tern_red, 2 * i + 2)
                link(d.tensor_scalar(t_[7], t_[4], 1.0 / (C * C * TAPS), None, ALU.mult))
                link(d.tensor_tensor(t_[8], t_[5], t_[7], ALU.subtract))
                link(d.tensor_scalar(t_[9], t_[6], -1.0, t_[7], ALU.mult, ALU.subtract))
                link(d.tensor_tensor(t_[10], t_[8], t_[9], ALU.subtract))
                link(d.tensor_scalar(t_[10], t_[10], 1.0 / 3.0, None, ALU.mult))
                d.tensor_tensor(t_[11], t_[9], t_[10], ALU.add)
                d.tensor_tensor(t_[12], t_[8], t_[10], ALU.subtract).then_inc(tern_th, 1)

            dve.wait_ge(consts, 6)
            dve.wait_ge(by_i, 2 * B)
            d.tensor_scalar(ci[:, 1:2], ci[:, 0:1], 5, None, ALU.logical_shift_right)
            link(d.tensor_scalar(ci[:, 2:3], ci[:, 0:1], W - 1, None, ALU.bitwise_and))
            d.tensor_copy(byf, byi.bitcast(I32))
            d.tensor_copy(rbf, rbi.bitcast(I32))
            d.tensor_copy(bxf[:, :], bxi[:, :])
            d.tensor_copy(colf[:, :], coli[:, :])
            link(d.tensor_copy(cf[:, 1:3], ci[:, 1:3]))
            d.tensor_scalar(bxf[:, :], bxf[:, :], cf[:, 2:3], None, ALU.add)
            d.tensor_scalar(rowj[:, :], colf[:, 0:NT], float(TR), cf[:, 1:2], ALU.mult, ALU.add)
            link(d.tensor_scalar(rbf, rbf, cf[:, 1:2], None, ALU.add))

            def positions(b):
                tiles = slice(b * NT, (b + 1) * NT)
                dve.wait_ge(off_ok, 4 * b + 4)
                o = omr[:, b * H:(b + 1) * H, :].rearrange("p (t a) c -> p t c a", a=TR)
                x_, y_, base = (m[:, tiles, :].rearrange("p t (k a) -> p t k a", a=TR) for m in (px, py, byf))
                d.tensor_tensor(x_, o[:, :, TAPS:2 * TAPS, :], bxf[:, :].unsqueeze(1).unsqueeze(3).to_broadcast([P, NT, TAPS, TR]),
                                ALU.add)
                link(d.tensor_tensor(y_, o[:, :, 0:TAPS, :], base, ALU.add))
                d.tensor_tensor(roww[:, tiles, :, 0], py[:, tiles, :], rbf[:, tiles, :], ALU.subtract)
                d.tensor_reduce(far[:, b:b + 1], omr[:, b * H:(b + 1) * H, 0:2 * TAPS], AX.XY, ALU.max,
                                apply_absolute_value=True)
                link(d.tensor_scalar(rbf[:, tiles, :], rbf[:, tiles, :], float(TR), None, ALU.add))
                d.tensor_tensor(roww[:, tiles, :, 1], py[:, tiles, :], rbf[:, tiles, :], ALU.subtract).then_inc(row_d, 1)

            def masked(b):
                tiles = slice(b * NT, (b + 1) * NT)
                dve.wait_ge(row_h, 2 * b + 2)
                dve.wait_ge(mask_ok, b + 1)
                d.tensor_tensor(roww[:, tiles, :, :], roww[:, tiles, :, :],
                                mask[:, tiles, :].unsqueeze(3).to_broadcast([P, NT, TAPS * TR, 2]), ALU.mult).then_inc(row_ok, 1)

            dve.wait_ge(boff_in, 16)
            for n in range(2 * B):
                dve.wait_ge(off_tail, n + 1)
                if n >= 2:
                    dve.wait_ge(off_t, n - 1)
                d.scalar_tensor_tensor(out=omh[:, n % 2, :], in0=Z_PS[n % 2][0:GRP, :], scalar=boffc[:, 0:1],
                                       in1=omt[:, n % 2, :], op0=ALU.add, op1=ALU.add).then_inc(off_sum, 1)
                dve.wait_ge(off_sum, n + 1)
                for g in range(2):
                    ins = d.transpose(omr[g * GRP:(g + 1) * GRP, n * H // 2:(n + 1) * H // 2, :].rearrange("p h c -> p (h c)"),
                                      omh[:, n % 2, :])
                ins.then_inc(off_t, 1)
                if n < 2:
                    thresholds(n)
                if n >= 2 and n % 2 == 0:
                    positions(n // 2 - 1)
                if n >= 3 and n % 2:
                    masked(n // 2 - 1)
            positions(B - 1)
            link(d.tensor_copy(cf[:, 0:1], cf[:, 1:2]))
            d.tensor_reduce(far[:, B:B + 1], far[:, 0:B], AX.X, ALU.max).then_inc(far_in, 1)
            masked(B - 1)
            dve.wait_ge(far_red, 1)
            d.tensor_scalar(fari[0:1, 0:1], far[0:1, B + 1:B + 2], float(REACH), None, ALU.is_le).then_inc(far_ok, 1)

            dve.sem_inc(s_ok, CREDIT)
            dve.wait_ge(far_ok, 1)
            near = dve.value_load(fari[0:1, 0:1], min_val=0, max_val=1)
            with dve.If(near == 1):
                def window(b, j, par):
                    for part, src in enumerate((xhi, xlo)):
                        d.tensor_copy(xwin[:, part, par, :, :],
                                      src[:, bass.ds(b * ROWS + j * TR, K + TR - 1), 1:1 + W]).then_inc(xw_ok, 1)

                def columns(tile, par):
                    d.tensor_tensor(hx[:, par, :, :],
                                    px[:, bass.ds(tile, 1), :].rearrange("p t n -> p (t n)").unsqueeze(2)
                                    .to_broadcast([P, TAPS * TR, W]),
                                    colf[:, :].unsqueeze(1).to_broadcast([P, TAPS * TR, W]), ALU.subtract).then_inc(hx_d, 1)

                def turn(b, s, par):
                    dve.wait_ge(v_ok, b * SLOTS + s + 1 + CREDIT)
                    dve.wait_ge(o_mm, b * SLOTS + s - 1 + CREDIT)
                    flat_ = "p n r w -> p (n r w)"
                    d.transpose(sq[:, par, :, :, :].rearrange(flat_), vt[:, par, :, :, :].rearrange(flat_)).then_inc(s_ok, 1)

                def pair(b, i, final):
                    for par in range(2):
                        for ky in range(K):
                            turn(b, 6 * i + K * par + ky, (par + ky) % 2)
                        if not (final and b == B - 1):
                            columns(b * NT + 2 * i + par + 2, par)
                        if not final:
                            dve.wait_ge(z_mm, b * ZPER + 6 * i + K * par + 2 * K + CREDIT)
                            window(b, 2 * i + par + 3, 1 - par)
                        elif b < B - 1:
                            if par == 0:
                                dve.wait_ge(z_mm, (b + 1) * ZPER + CREDIT)
                                window(b + 1, 0, 0)
                                window(b + 1, 1, 1)
                            else:
                                dve.wait_ge(z_mm, (b + 1) * ZPER + 5 + CREDIT)
                                window(b + 1, 2, 0)

                window(0, 0, 0)
                window(0, 1, 1)
                for par in range(2):
                    columns(par, par)
                dve.wait_ge(z_mm, 5 + CREDIT)
                window(0, 2, 0)
                for b in range(B):
                    with dve.Fori(0, NT // 2 - 1) as i:
                        pair(b, i, False)
                    pair(b, NT // 2 - 1, True)
            with dve.Else():
                dve.wait_ge(vec_in, 7 * 16)
                d.memset(ysb[:, :, :], 0.0).then_inc(any_ok, 1)
                dve.wait_ge(any_ok, 1)
                d.tensor_scalar(ysb[:, :, :], ysb[:, :, :], v_bias, None, ALU.add).then_inc(any_ok, 1)
                dve.wait_ge(any_ok, 2)
                hf = hx[:, :, :, :].rearrange("p a n w -> p (a n w)")
                cols = [hf[:, m * NT * P:(m + 1) * NT * P].rearrange("p (n w) -> p n w", w=W) for m in range(2)]
                rows = [rowany[:, m, :, :] for m in range(2)]

                with dve.Fori(0, B) as b:
                    with dve.Fori(0, TAPS) as k:
                        it = b * TAPS + k
                        done = [0]

                        def step(ins, last=True):
                            done[0] += 1
                            ins.then_inc(any_ok, 1)
                            dve.wait_ge(any_ok, it * 7 + 2 + done[0])

                        for j in range(NT):
                            dve.wait_ge(z_mm, it * NT + j - 1 + CREDIT)
                            for part, src in enumerate((xhi, xlo)):
                                d.tensor_copy(xwin[:, part, j % 2, 0:TR, :],
                                              src[:, bass.ds(b * ROWS + TOP + j * TR, TR), 1:1 + W]).then_inc(xw_ok, 1)
                        at = (slice(None), bass.ds(b * NT, NT), bass.ds(k * TR, TR))
                        for m, pos, n in ((cols, px, W), (rows, py, NT)):
                            p_ = pos[at].unsqueeze(3).to_broadcast([P, NT, TR, n])
                            q_ = (colf[:, :] if n == W else rowj[:, :]).unsqueeze(1).unsqueeze(1).to_broadcast([P, NT, TR, n])
                            m0, m1 = (x_.rearrange("p (t a) w -> p t a w", a=TR) for x_ in m)
                            d.tensor_tensor(m0, p_, q_, ALU.subtract)
                            step(d.tensor_tensor(m1, q_, p_, ALU.subtract))
                            step(d.tensor_tensor(m[0], m[0], m[1], ALU.max))
                            step(d.tensor_scalar(m[0], m[0], 1.0, -1.0, ALU.min, ALU.add))
                        step(d.tensor_tensor(rows[0].rearrange("p (t a) w -> p t a w", a=TR),
                                             rows[0].rearrange("p (t a) w -> p t a w", a=TR),
                                             mask[at].unsqueeze(3).to_broadcast([P, NT, TR, NT]), ALU.mult))
                        for pt in range(NT):
                            for half in range(2):
                                n = (it * NT + pt) * 2 + half
                                r_ = rows[0][:, pt * TR:(pt + 1) * TR, 4 * half:4 * half + 4].rearrange("p a j -> p j a")
                                c_ = cols[0][:, pt * TR:(pt + 1) * TR, :]
                                d.tensor_tensor(sany(vt, half).rearrange("p j (a w) -> p j a w", w=W),
                                                r_.unsqueeze(3).to_broadcast([P, 4, TR, W]),
                                                c_.unsqueeze(1).to_broadcast([P, 4, TR, W]), ALU.mult).then_inc(v_ok, 1)
                                dve.wait_ge(v_ok, n + 1 + CREDIT)
                                dve.wait_ge(o_mm, it * NT + pt + CREDIT)
                                d.transpose(sany(sq, half).rearrange("p j n -> p (j n)"),
                                            sany(vt, half).rearrange("p j n -> p (j n)")).then_inc(s_ok, 1)
                            dve.wait_ge(o_mm, it * NT + pt + 1 + CREDIT)
                            y = ysb[:, bass.ds(b, 1), pt * P:(pt + 1) * P].rearrange("p a n -> p (a n)")
                            d.tensor_tensor(y, y, O_PS[pt % 2][:, 0:P], ALU.add).then_inc(y_ok, 1)

            dve.wait_ge(y_done, 1)
            image_stats(GN8, ysb, None)
            normalise(GN8, (1, Z_PS[0][:, 0:B], Z_PS[1][:, 0:B]), v_gamma, v_beta)
            for b in range(B):
                dve.wait_ge(y_norm, b + 1)
                d.tensor_tensor(xs[:, b, 256:HW], xs[:, b, 256:HW], ysb[:, b, 256:HW], ALU.add).then_inc(x1_ok, 1)
            image_stats(GN1, xs, lambda b: dve.wait_ge(x1_ok, 2 * B))
            normalise(GN1, (2, O_PS[0][:, 0:B], O_PS[1][:, 0:B]), None, None)
            tails(GN1, B)

            def conv_stats(n, done):
                for m in range(2 * B):
                    dve.wait_ge(done, m + 1)
                    ins = d.bn_stats(st[:, n, m, :], PS[:, m, :])
                link(ins)
                link(d.bn_aggr(mv[:, n, 0, :], st[:, n, :, :]))

            conv_stats(BN1, c1_mm)
            normalise(BN1, None, v_g1, v_be1)
            for n in range(2 * B):
                b, h = n // 2, n % 2
                dve.wait_ge(r1_ok, n + 1)
                rows = slice(b * ROWS + TOP + h * 16, b * ROWS + TOP + h * 16 + 16)
                v = square(r1[:, b, h * BIG:(h + 1) * BIG])
                d.tensor_copy(xhi[:, rows, 1:1 + W], v).then_inc(r1hi_ok, 1)
                dve.wait_ge(r1hi_ok, n + 1)
                d.tensor_tensor(xlo[:, rows, 1:1 + W], v, xhi[:, rows, 1:1 + W], ALU.subtract).then_inc(r1lo_ok, 1)
            conv_stats(BN2, c2_mm)
            normalise(BN2, None, v_g2, v_be2)

            def finish(n):
                dve.wait_ge(f_relu, n + 1)
                v = slice((n % 2) * BIG, (n % 2 + 1) * BIG)
                d.tensor_tensor(ysb[:, n // 2, v], ysb[:, n // 2, v], xs[:, n // 2, v], ALU.add).then_inc(f_ok, 1)

            for n in range(2 * B):
                v = slice((n % 2) * BIG, (n % 2 + 1) * BIG)
                d.scalar_tensor_tensor(out=ysb[:, n // 2, v], in0=PS[:, n, :], scalar=scale_of(BN2, 0),
                                       in1=r1[:, n // 2, v], op0=ALU.mult, op1=ALU.add).then_inc(f_sum, 1)
                if n >= 2:
                    finish(n - 2)
            finish(2 * B - 2)
            finish(2 * B - 1)


_INS = ["x", "L0_conv_w_off", "L0_conv_b_off", "L0_conv_weight", "L0_conv_bias", "L0_conv_gamma", "L0_conv_beta",
        "L1_conv_w1", "L1_conv_gamma1", "L1_conv_beta1", "L1_conv_w2", "L1_conv_gamma2", "L1_conv_beta2"]


def kernel(**inputs):
    import numpy as np
    import concourse.bacc as bacc
    from concourse.bass_utils import run_bass_kernel_spmd

    nc = bacc.Bacc("TRN2", target_bir_lowering=False, num_devices=1)
    arrays, args = {}, []
    for name in _INS:
        arrays[f"in_{name}"] = a = np.ascontiguousarray(inputs[name])
        args.append(nc.dram_tensor(f"in_{name}", a.shape, mybir.dt.from_np(a.dtype), kind="ExternalInput").ap())
    out = nc.dram_tensor("out", (B, C, H, W), F32, kind="ExternalOutput").ap()
    build(nc, *args, out)
    r = run_bass_kernel_spmd(nc, [arrays], core_ids=[0])
    return r.results[0]["out"]
```

```python
from contextlib import ExitStack

import concourse.bass as bass
from concourse import mybir

F32 = mybir.dt.float32
F32R = mybir.dt.float32r
I32 = mybir.dt.int32
ALU = mybir.AluOpType
ACT = mybir.ActivationFunctionType
AX = mybir.AxisListType

B, C, H, W = 4, 128, 32, 32
P = 128
K = 3
TAPS = K * K
HW = H * W
TR = P // W
NT = HW // P
REACH = 2
WIN = 2 * TR
TOP = REACH + 1
ROWS = H + TR
PROWS = B * ROWS + 2
PW = W + 2
OFFC = 3 * TAPS
GRP = 32
NG = P // GRP
TILES = B * NT
EPS = 1e-5
SLOTS = NT * K
ZPER = (NT + 1) * K
FOLDS = 4
BIG = 512


def build(nc, x, w_off, b_off, wd, bias, gamma, beta, w1, g1, be1, w2, g2, be2, out):
    x_v = x.rearrange("b c h w -> c b (h w)")
    out_v = out.rearrange("b c h w -> c b (h w)")
    flat = "o c h w -> o (c h w)"

    with ExitStack() as ctx:
        def sb(name, shape, dt=F32):
            return ctx.enter_context(nc.sbuf_tensor(name, shape, dt))

        def sem(name):
            return ctx.enter_context(nc.semaphore(name))

        GN0, GN8, GN1, BN1, BN2 = range(5)

        xs = sb("xs", [P, B, HW])
        xhi = sb("xhi", [P, PROWS, PW], F32R)
        xlo = sb("xlo", [P, PROWS, PW], F32R)
        ysb = sb("ysb", [P, B, HW])
        r1 = sb("r1", [P, B, HW])
        hx = sb("hx", [P, 2, TAPS * TR, W])
        roww = sb("roww", [P, TILES, TAPS * TR, 2])
        woff_raw = sb("woff_raw", [OFFC, C * TAPS])
        wd_raw = sb("wd_raw", [P, C * TAPS])
        woffT = sb("woffT", [P, TAPS, P], F32R)
        wdhi = sb("wdhi", [P, TAPS, P], F32R)
        wdlo = sb("wdlo", [P, TAPS, P], F32R)
        q1 = sb("q1", [P, TAPS, P], F32R)
        q2 = sb("q2", [P, TAPS, P], F32R)
        omt = sb("omt", [GRP, 2, BIG])
        omh = sb("omh", [GRP, 2, BIG])
        omr = sb("omr", [P, B * H, GRP])
        xwin = sb("xwin", [P, 2, 2, K + TR - 1, W], F32R)
        zr = sb("zr", [P, 2, K, K, P])
        vt = sb("vt", [P, 2, K * TR, 2, W])
        sq = sb("sq", [P, 2, K * TR, 2, W])
        ident = sb("ident", [P, P])
        g32 = sb("g32", [P, P])
        g16 = sb("g16", [P, P])
        boffc = sb("boffc", [GRP, 1])
        warm = sb("warm", [GRP, 1])
        vec = sb("vec", [P, 8])
        ci = sb("ci", [P, 4], I32)
        cf = sb("cf", [P, 4])
        bxi = sb("bxi", [P, TAPS], I32)
        bxf = sb("bxf", [P, TAPS])
        coli = sb("coli", [P, W], I32)
        colf = sb("colf", [P, W])
        rowj = sb("rowj", [P, NT])
        px = sb("px", [P, TILES, TAPS * TR])
        py = sb("py", [P, TILES, TAPS * TR])
        mask = sb("mask", [P, TILES, TAPS * TR])
        rowany = sb("rowany", [P, 2, NT * TR, NT])
        st = sb("st", [P, 5, 2 * B, 6])
        mv = sb("mv", [P, 5, B, 2])
        nsm = sb("nsm", [P, 5, 10, B])
        tw = sb("tw", [P, 2, 16])
        far = sb("far", [P, B + 2])
        fari = sb("fari", [1, 1], I32)
        r1f = r1[:, :, :].rearrange("p b n -> p (b n)")
        wraw = [r1f[:, i * C * TAPS:(i + 1) * C * TAPS] for i in range(2)]
        wscr = r1f[:, 2 * C * TAPS:3 * C * TAPS]
        fold = [wscr[:, m * C * TAPS // 2:(m + 1) * C * TAPS // 2] for m in range(2)]
        zf = ysb[:, B - 1, :]
        byf, rbf, rbf2 = (zf[:, i * NT * TAPS * TR:(i + 1) * NT * TAPS * TR].rearrange("p (t n) -> p t n", t=NT)
                    for i in range(3))
        byi, rbi = (m[:, :, :, :, :].rearrange("p a b c w -> p (a b c w)")[:, 0:NT * TAPS * TR]
                    .rearrange("p (t n) -> p t n", t=NT) for m in (vt, sq))
        zany = omr[:, 0:HW // GRP, :].rearrange("p h c -> p (h c)")
        xn = {GN0: omr[:, :, :].rearrange("p (b h) c -> p b (h c)", b=B), GN1: ysb}

        PS = ctx.enter_context(nc.psum_tensor("PS", [P, 2 * B, BIG], F32))
        Z_PS = [PS[:, 4, :], PS[:, 5, :]]
        ZB_PS = [PS[:, 2, :], PS[:, 3, :]]
        O_PS = [PS[:, 6, :], PS[:, 7, :]]
        DVE_CHUNKS, POOL_CHUNKS = range(0, 2 * B, 2), range(1, 2 * B, 2)
        OUT_ORDER = (0, 2, 1, 4, 3, 6, 5, 7)
        OFF_PS = [PS[:, 4 + m, :] for m in range(4)]

        x_in = [sem(f"x_in{b}") for b in range(B)]
        woff_in, wd_in, w1_in, w2_in, vec_in, boff_in = (
            sem(n) for n in ("woff_in", "wd_in", "w1_in", "w2_in", "vec_in", "boff_in"))
        gps = sem("gps")
        consts = sem("consts")
        dch = sem("dch")
        pads = sem("pads")
        zeroed = sem("zeroed")
        gn_in, gn_mean, gn_dev, gn_msq, gn_var, gn_std = (
            sem(n) for n in ("gn_in", "gn_mean", "gn_dev", "gn_msq", "gn_var", "gn_std"))
        gn_ok = sem("gn_ok")
        xhi_ok, xlo_ok = sem("xhi_ok"), sem("xlo_ok")
        woff_t, woff_hi, woff_ok = sem("woff_t"), sem("woff_hi"), sem("woff_ok")
        wd_t, wd_hi, wd_ok = sem("wd_t"), sem("wd_hi"), sem("wd_ok")
        off_mm, off_tail, off_sum, off_t, off_ok = (sem(n) for n in ("off_mm", "off_tail", "off_sum", "off_t", "off_ok"))
        by_i, base_ok = sem("by_i"), sem("base_ok")
        pos_ok, mask_ok, row_d, row_h, row_ok = (sem(n) for n in ("pos_ok", "mask_ok", "row_d", "row_h", "row_ok"))
        far_in, far_red, far_ok = sem("far_in"), sem("far_red"), sem("far_ok")
        tern_in, tern_red, tern_th, tern_c, tern_ok = (
            sem(n) for n in ("tern_in", "tern_red", "tern_th", "tern_c", "tern_ok"))
        tern_fold, tern_min, tern_s = sem("tern_fold"), sem("tern_min"), sem("tern_s")
        q_t, q_ok = sem("q_t"), sem("q_ok")
        hx_d, hx_a, hx_ok = sem("hx_d"), sem("hx_a"), sem("hx_ok")
        v_ok, s_ok = sem("v_ok"), sem("s_ok")
        xw_ok, z_mm, z_ok = sem("xw_ok"), sem("z_mm"), sem("z_ok")
        o_mm, y_ok = sem("o_mm"), sem("y_ok")
        any_ok = sem("any_ok")
        y_done = sem("y_done")
        y_norm, x1_ok, xn_ok = sem("y_norm"), sem("x1_ok"), sem("xn_ok")
        c1_mm, c2_mm = sem("c1_mm"), sem("c2_mm")
        r1_ok, r1hi_ok, r1lo_ok = sem("r1_ok"), sem("r1hi_ok"), sem("r1lo_ok")
        rx_ok, f_scaled, f_act, f_sum, f_relu, out_done = (
            sem(n) for n in ("rx_ok", "f_scaled", "f_act", "f_sum", "f_relu", "out_done"))
        out_ok = [sem(f"out_ok{n}") for n in range(2 * B)]

        CREDIT = 2
        PRIMED = CREDIT + 2 * K
        v_bias, v_gamma, v_beta, v_g1, v_be1, v_g2, v_be2 = (vec[:, i:i + 1] for i in range(7))

        def order(n, b):
            return {GN0: min(b, 1), GN8: 2 + 2 * b, GN1: 3 + 2 * b, BN1: 2 + 2 * B, BN2: 3 + 2 * B}[n]

        IN_LOOP = [(n, b) for b in range(B - 1) for n in (GN8, GN1) if (n, b) != (GN1, B - 2)]

        def images(n, b):
            return slice(b, B if n == GN0 and b else b + 1)

        def group_sums(n, b):
            bank = {GN0: 6, GN8: 4 if b == B - 1 else 0, GN1: 1 if b < B - 2 else 5 + b - (B - 2)}[n]
            at = images(n, b)
            return PS[:, bank, at], PS[:, bank, B + at.start:B + at.stop]

        def scale_of(n, b):
            return nsm[:, n, 8, b:b + 1]

        def shift_of(n, b):
            return nsm[:, n, 9, b:b + 1]

        def inner(img, b):
            return img[:, b * ROWS + TOP:b * ROWS + TOP + H, 1:1 + W]

        def sany(m, half):
            return m[:, half, :, :, :].rearrange("p n r w -> p (n r w)")[:, 0:4 * P].rearrange("p (j n) -> p j n", j=4)

        def chunk(m, n):
            return m[:, n // 2, (n % 2) * BIG:(n % 2 + 1) * BIG]

        def chunk_rows(img, n):
            r = n // 2 * ROWS + TOP + (n % 2) * (H // 2)
            return img[:, r:r + H // 2, 1:1 + W]

        def square(a):
            return a.rearrange("p (h w) -> p h w", w=W)

        block = ctx.enter_context(nc.Block())

        @block.sync
        def _(sp):
            for b in range(B):
                sp.dma_start(xs[:, b, :], x_v[:, b, :]).then_inc(x_in[b], 16)
            sp.dma_start(wraw[0], w1.rearrange(flat)).then_inc(w1_in, 16)
            sp.dma_start(wraw[1], w2.rearrange(flat)).then_inc(w2_in, 16)
            for i, v in enumerate((bias, gamma, beta, g1, be1, g2, be2)):
                sp.dma_start(vec[:, i:i + 1], v.rearrange("(c a) -> c a", a=1)).then_inc(vec_in, 16)
            for n in OUT_ORDER:
                sp.wait_ge(out_ok[n], 1)
                sp.dma_start(out_v[:, n // 2, (n % 2) * BIG:(n % 2 + 1) * BIG],
                             ysb[:, n // 2, (n % 2) * BIG:(n % 2 + 1) * BIG]).then_inc(out_done, 16)
            sp.wait_ge(out_done, 16 * 2 * B)

        @block.gpsimd
        def _(pool):
            g = nc.gpsimd
            g.memset(ident[:, :], 1.0).then_inc(gps, 1)
            g.memset(g32[:, :], 0.25).then_inc(gps, 1)
            g.memset(g16[:, :], 0.125).then_inc(gps, 1)
            pool.wait_ge(gps, 3)
            g.affine_select(out=ident[:, :], in_=ident[:, :], compare_op=ALU.is_equal, fill=0.0, base=0,
                            pattern=[[-1, P]], channel_multiplier=1).then_inc(consts, 1)
            for m, n in ((g32, 4), (g16, 8)):
                v = m[:, :].rearrange("p (g n) -> p g n", n=n)
                g.affine_select(out=v, in_=v, compare_op=ALU.is_ge, fill=0.0, base=0,
                                pattern=[[-n, P // n], [0, n]], channel_multiplier=1).then_inc(gps, 1)
            pool.wait_ge(gps, 5)
            for m, n in ((g32, 4), (g16, 8)):
                v = m[:, :].rearrange("p (g n) -> p g n", n=n)
                g.affine_select(out=v, in_=v, compare_op=ALU.is_ge, fill=0.0, base=n - 1,
                                pattern=[[n, P // n], [0, n]], channel_multiplier=-1).then_inc(consts, 1)
            for img in (xhi, xlo):
                m = img[:, :, :].bitcast(F32)
                by_image = m[:, 0:B * ROWS, :].rearrange("p (b r) w -> p b r w", b=B)
                for border in (by_image[:, :, 0:TOP, :], by_image[:, :, TOP + H:ROWS, :], m[:, B * ROWS:PROWS, :],
                               by_image[:, :, TOP:TOP + H, 0:PW:PW - 1]):
                    g.memset(border, 0.0).then_inc(pads, 1)
            g.iota(ci[:, 0:1], [[0, 1]], base=0, channel_multiplier=1).then_inc(consts, 1)
            g.iota(bxi[:, :], [[0, K], [1, K]], base=-1, channel_multiplier=0).then_inc(consts, 1)
            g.iota(coli[:, :], [[1, W]], base=0, channel_multiplier=0).then_inc(consts, 1)
            for m, top, row in ((byi, -1, 1), (rbi, -TOP, 0)):
                g.iota(m.bitcast(I32), [[TR, NT], [1, K], [0, K], [row, TR]], base=top, channel_multiplier=0).then_inc(by_i, 1)
            for i, arrived in enumerate((w1_in, w2_in)):
                pool.wait_ge(arrived, 16)
                n = C * TAPS
                for level in range(FOLDS):
                    src = wraw[i] if level == 0 else fold[i]
                    n //= 2
                    g.tensor_tensor(fold[i][:, 0:n], src[:, 0:n], src[:, n:2 * n], ALU.add).then_inc(tern_fold, 1)
                    pool.wait_ge(tern_fold, FOLDS * i + level + 1)

            def positions(b, step):
                tiles = slice(b * NT, (b + 1) * NT)
                o = omr[:, b * H:(b + 1) * H, :].rearrange("p (t a) c -> p t c a", a=TR)
                x_, y_, base = (m.rearrange("p t (k a) -> p t k a", a=TR) for m in (px[:, tiles, :], py[:, tiles, :], byf))
                if step == 0:
                    pool.wait_ge(off_ok, 4 * b + 4)
                    g.tensor_tensor(y_, o[:, :, 0:TAPS, :], base, ALU.add).then_inc(pos_ok, 1)
                elif step == 1:
                    g.tensor_tensor(x_, o[:, :, TAPS:2 * TAPS, :],
                                    bxf[:, :].unsqueeze(1).unsqueeze(3).to_broadcast([P, NT, TAPS, TR]), ALU.add).then_inc(pos_ok, 1)
                else:
                    pool.wait_ge(pos_ok, 2 * b + 1)
                    g.tensor_tensor(roww[:, tiles, :, step - 2], py[:, tiles, :], (rbf, rbf2)[step - 2],
                                    ALU.subtract).then_inc(row_d, 1)

            for i in range(2):
                pool.wait_ge(tern_in, i + 1)
                g.partition_all_reduce(tw[:, i, 4:5], tw[:, i, 0:1], P, bass.bass_isa.ReduceOp.add).then_inc(tern_red, 1)
                g.partition_all_reduce(tw[:, i, 5:7], tw[:, i, 1:3], P, bass.bass_isa.ReduceOp.max).then_inc(tern_red, 1)
                mean, top, low, third, upper, lower, neg_mean = (tw[:, i, m:m + 1] for m in (7, 8, 9, 10, 12, 11, 13))
                pool.wait_ge(tern_red, 2 * i + 2)
                g.tensor_scalar(mean, tw[:, i, 4:5], 1.0 / (C * C * TAPS), None, ALU.mult).then_inc(tern_s, 1)
                g.tensor_scalar(low, tw[:, i, 6:7], -1.0, None, ALU.mult).then_inc(tern_s, 1)
                pool.wait_ge(tern_s, 7 * i + 2)
                g.tensor_tensor(top, tw[:, i, 5:6], mean, ALU.subtract).then_inc(tern_s, 1)
                g.tensor_tensor(low, low, mean, ALU.subtract).then_inc(tern_s, 1)
                g.tensor_scalar(neg_mean, mean, -1.0, None, ALU.mult).then_inc(tern_s, 1)
                pool.wait_ge(tern_s, 7 * i + 5)
                g.tensor_tensor(third, top, low, ALU.subtract).then_inc(tern_s, 1)
                pool.wait_ge(tern_s, 7 * i + 6)
                g.tensor_scalar(third, third, 1.0 / 3.0, None, ALU.mult).then_inc(tern_s, 1)
                pool.wait_ge(tern_s, 7 * i + 7)
                g.tensor_tensor(lower, low, third, ALU.add).then_inc(tern_th, 1)
                g.tensor_tensor(upper, top, third, ALU.subtract).then_inc(tern_th, 1)
            pool.wait_ge(base_ok, 1)
            for b in range(B - 1):
                for step in range(4):
                    positions(b, step)
            pool.wait_ge(far_in, 1)
            g.partition_all_reduce(far[:, B + 1:B + 2], far[:, B:B + 1], P, bass.bass_isa.ReduceOp.max).then_inc(far_red, 1)

            def add_y(b, h):
                pool.wait_ge(y_norm, b + 1)
                g.tensor_tensor(chunk(xs, 2 * b + h), chunk(xs, 2 * b + h), chunk(ysb, 2 * b + h), ALU.add).then_inc(x1_ok, 1)

            pool.sem_inc(v_ok, CREDIT)
            pool.wait_ge(far_ok, 1)
            near = pool.value_load(fari[0:1, 0:1], min_val=0, max_val=1)
            with pool.If(near == 1):
                def outer(b, i, u):
                    tile, ky, par = b * NT + 2 * i + u // K, u % K, u // K
                    if ky == 0:
                        pool.wait_ge(hx_ok, tile + 1)
                    pool.wait_ge(s_ok, b * SLOTS + 6 * i + u - 1 + CREDIT)
                    n = K * TR
                    rows = roww[:, bass.ds(tile, 1), n * ky:n * ky + n, :].rearrange("p t n r -> p (t n) r")
                    g.tensor_tensor(vt[:, u % 2, :, :, :], rows.unsqueeze(3).to_broadcast([P, n, 2, W]),
                                    hx[:, par, n * ky:n * ky + n, :].unsqueeze(2).to_broadcast([P, n, 2, W]),
                                    ALU.mult).then_inc(v_ok, 1)

                for b in range(B):
                    pool.wait_ge(row_ok, b + 1)
                    if b == 0:
                        for i in range(2):
                            for u in range(6):
                                outer(0, i, u)
                                if u in (2, 5):
                                    positions(B - 1, 2 * i + u // 3)
                    with pool.Fori(0 if b else 2, NT // 2 - 1 if b else NT // 2) as i:
                        for u in range(6):
                            outer(b, i, u)
                    if b:
                        for u in range(6):
                            outer(b, NT // 2 - 1, u)
                            if b < B - 1 and u in (3, 4):
                                add_y(b - 1, u - 3)
                for h in range(2):
                    add_y(B - 2, h)
            with pool.Else():
                for step in range(2):
                    positions(B - 1, step)
                for b in range(B - 1):
                    for h in range(2):
                        add_y(b, h)

            for n in DVE_CHUNKS:
                pool.wait_ge(r1_ok, n + 1)
                g.tensor_tensor(chunk(ysb, n), chunk(r1, n), chunk(xs, n), ALU.add).then_inc(rx_ok, 1)
            for m, n in enumerate(POOL_CHUNKS):
                pool.wait_ge(f_act, m + 1)
                g.tensor_tensor(chunk(ysb, n), chunk(ysb, n), chunk(r1, n), ALU.add).then_inc(f_sum, 1)
            pool.wait_ge(f_relu, B)
            g.tensor_tensor(chunk(ysb, n), chunk(ysb, n), chunk(xs, n), ALU.add).then_inc(out_ok[n], 1)

        @block.tensor
        def _(pe):
            t = nc.tensor
            pe.wait_ge(consts, 3)
            pe.wait_ge(woff_in, 16)
            v = woff_raw[:, :].rearrange("o (c k) -> o k c", k=TAPS)
            for k in range(TAPS):
                last = t.transpose(PS[:, 0, k * OFFC:(k + 1) * OFFC], v[:, k, :], ident[0:OFFC, 0:OFFC])
            last.then_inc(woff_t, 1)

            def turn_deformable(m):
                if m == 0:
                    pe.wait_ge(wd_in, 16)
                v = wd_raw[:, :].rearrange("o (c k) -> o k c", k=TAPS)
                for k in range(K * m, K * m + K):
                    last = t.transpose(PS[:, 1 + m, (k % K) * P:(k % K + 1) * P], v[:, k, :], ident[:, :])
                last.then_inc(wd_t, 1)

            def group_mean(n, b):
                pe.wait_ge(gn_in, order(n, b) + 1)
                t.matmul(group_sums(n, b)[0], (g16 if n == GN8 else g32)[:, :], mv[:, n, images(n, b), 0],
                         start=True, stop=True).then_inc(gn_mean, 1)

            def group_square(n, b):
                pe.wait_ge(gn_dev, order(n, b) + 1)
                t.matmul(group_sums(n, b)[1], (g16 if n == GN8 else g32)[:, :], nsm[:, n, 1, images(n, b)],
                         start=True, stop=True).then_inc(gn_msq, 1)

            group_mean(GN0, 0)
            group_square(GN0, 0)
            turn_deformable(0)
            turn_deformable(1)
            turn_deformable(2)

            pe.wait_ge(woff_ok, 1)
            pe.wait_ge(pads, 8)
            for b in range(B):
                pe.wait_ge(xhi_ok, b + 1)
                for h in range(2):
                    if b >= 2:
                        pe.wait_ge(off_sum, 2 * b + h - 3)
                    for part, src in enumerate((xhi, xlo)):
                        if part:
                            pe.wait_ge(xlo_ok, b + 1)
                        for k in range(TAPS):
                            r = b * ROWS + TOP - 1 + h * (H // 2) + k // K
                            last = t.matmul(OFF_PS[(2 * b + h) % 4], woffT[:, k, :], src[:, r:r + H // 2, k % K:k % K + W],
                                            start=(k == 0 and part == 0), stop=(k == TAPS - 1 and part == 1))
                            if (b, h, part, k) == (0, 0, 1, 4):
                                group_mean(GN0, 1)
                            if (b, h, part, k) == (0, 1, 0, 2):
                                group_square(GN0, 1)
                    last.then_inc(off_mm, 1)

            for s in (z_mm, o_mm):
                pe.sem_inc(s, CREDIT)

            def z_block(bank, par, ky, w_taps):
                n = w_taps(wdhi)
                win = [xwin[:, part, par, ky:ky + TR, :].rearrange("p r w -> p (r w)") for part in range(2)]
                dst = bank[:, 0:n.shape[-1]]
                t.matmul(dst, win[0], n, start=True, stop=False)
                t.matmul(dst, win[1], n, start=False, stop=False)
                t.matmul(dst, win[0], w_taps(wdlo), start=False, stop=True).then_inc(z_mm, 1)

            def taps_of(ky):
                return lambda w: w[:, K * ky:K * ky + K, :].rearrange("p k o -> p (k o)")

            def seam(b, ky):
                if ky == 0:
                    pe.wait_ge(xw_ok, (b * (NT + 1) + 2) * 2)
                if b or ky == K - 1:
                    pe.wait_ge(z_ok, b * ZPER - 1 + ky + CREDIT)
                z_block(Z_PS[(ky + 1) % 2], 0, ky, taps_of(ky))
                if ky == K - 1:
                    pe.wait_ge(z_ok, b * ZPER + 2 + CREDIT)
                z_block(ZB_PS[ky % 2], 1, ky, taps_of(ky))

            pe.wait_ge(wd_hi, K)
            pe.wait_ge(wd_ok, K)
            pe.wait_ge(off_sum, 2 * B - 2)
            for ky in range(K):
                seam(0, ky)

            def turn_weights(m):
                if m:
                    pe.wait_ge(q_ok, 2 * m)
                for i in (2 * m, 2 * m + 1):
                    pe.wait_ge(tern_ok, i // K + 1)
                    v = wraw[i // K].rearrange("o (c k) -> o k c", k=TAPS)
                    for k in range(K):
                        last = t.transpose(ZB_PS[i % 2][:, k * P:(k + 1) * P], v[:, i % K * K + k, :], ident[:, :])
                    last.then_inc(q_t, 1)

            def meanwhile(b, final, u):
                if not final and b:
                    if b == 1 and u in (1, 3, 5):
                        if u == 1:
                            pe.wait_ge(z_ok, b * ZPER + 2 * K + CREDIT)
                        turn_weights(u // 2)
                    if b >= 2 and u in (1, 3):
                        (group_mean if u == 1 else group_square)(GN1, b - 2)
                    if u in (2, 4):
                        (group_mean if u == 2 else group_square)(GN8, b - 1)
                if final and b == 1 and u == 0:
                    pe.wait_ge(q_ok, 2 * K)

            pe.wait_ge(far_ok, 1)
            pe.wait_ge(off_sum, 2 * B)
            near = pe.value_load(fari[0:1, 0:1], min_val=0, max_val=1)
            with pe.If(near == 1):
                def multiply(b, s, par, ky, spar, pt, z):
                    pe.wait_ge(s_ok, b * SLOTS + s + 1 + CREDIT)
                    pe.wait_ge(z_ok, b * ZPER + z + CREDIT)
                    if ky == 0:
                        pe.wait_ge(y_ok, b * NT + pt - 1 + CREDIT)
                    for kx in range(K):
                        for blk in range(2):
                            last = t.matmul(O_PS[par][:, 0:P], zr[:, (par + blk) % 2, ky, kx, :],
                                            sq[:, spar, TR * kx:TR * kx + TR, blk, :],
                                            start=(ky == 0 and kx == 0 and blk == 0),
                                            stop=(ky == K - 1 and kx == K - 1 and blk == 1))
                    last.then_inc(o_mm, 1)

                def pair(b, i, first=False, final=False):
                    for par in range(2):
                        for ky in range(K):
                            u = K * par + ky
                            if first or final:
                                meanwhile(b, final, u)
                            pt, z = 2 * i + par, 6 * i + u + 6
                            if not (final and par == 1):
                                if ky == 0:
                                    pe.wait_ge(xw_ok, (b * (NT + 1) + pt + 3) * 2)
                                pe.wait_ge(z_ok, b * ZPER + (z - 1 if not first or u > 1 else (3, 5)[u]) + CREDIT)
                                z_block(Z_PS[u % 2], par, ky, taps_of(ky))
                            elif b < B - 1:
                                seam(b + 1, ky)
                            multiply(b, 6 * i + u, par, ky, u % 2, pt, 2 * ky + 2 if first and par == 0 else z - 2)

                for b in range(B):
                    pair(b, 0, first=True)
                    with pe.Fori(1, NT // 2 - 1) as i:
                        pair(b, i)
                    pair(b, NT // 2 - 1, final=True)
            with pe.Else():
                with pe.Fori(0, B) as b:
                    with pe.Fori(0, TAPS) as k:
                        it = b * TAPS + k
                        for j in range(NT):
                            pe.wait_ge(xw_ok, (it * NT + j + 1 + 3) * 2)
                            pe.wait_ge(z_ok, it * NT + j - 1 + PRIMED)
                            z_block(Z_PS[j % 2], j % 2, 0, lambda w: w[:, bass.ds(k, 1), :].rearrange("p k o -> p (k o)"))
                        with pe.Fori(0, NT // 2) as i:
                            for par in range(2):
                                pe.wait_ge(z_ok, (it + 1) * NT + PRIMED)
                                pe.wait_ge(y_ok, it * NT + 2 * i + par - 1 + CREDIT)
                                for j in range(NT):
                                    if j % 4 == 0:
                                        pe.wait_ge(s_ok, (it * NT + 2 * i + par) * 2 + j // 4 + 1 + CREDIT)
                                    last = t.matmul(O_PS[par][:, 0:P], zany[:, j * P:(j + 1) * P], sany(sq, j // 4)[:, j % 4, :],
                                                    start=(j == 0), stop=(j == NT - 1))
                                last.then_inc(o_mm, 1)

                for n, b in IN_LOOP:
                    group_mean(n, b)
                    group_square(n, b)
                for m in range(K):
                    turn_weights(m)

            def conv(q, b, h, done, hi, lo, n, between=None):
                for part, (src, ready) in enumerate(((xhi, hi), (xlo, lo))):
                    pe.wait_ge(ready, n)
                    if part and between is not None:
                        between()
                    for k in range(TAPS):
                        r = b * ROWS + TOP - 1 + h * (H // 2) + k // K
                        last = t.matmul(PS[:, bass.ds(2 * b + h, 1), :].rearrange("p a n -> p (a n)"), q[:, k, :],
                                        src[:, bass.ds(r, H // 2), k % K:k % K + W],
                                        start=(k == 0 and part == 0), stop=(k == TAPS - 1 and part == 1))
                last.then_inc(done, 1)

            pe.wait_ge(q_ok, 2 * K)

            def sums(group):
                for n, b in ((GN1, B - 2), (GN8, B - 1)):
                    group(n, b)

            for n in range(2 * B):
                b, h = n // 2, n % 2
                if n == 1:
                    sums(group_mean)
                conv(q1, b, h, c1_mm, xhi_ok, xlo_ok, B + b + 1,
                     {1: lambda: sums(group_square), 3: lambda: group_mean(GN1, B - 1),
                      4: lambda: group_square(GN1, B - 1)}.get(n))
            with pe.Fori(0, B) as b:
                for h in range(2):
                    conv(q2, b, h, c2_mm, r1hi_ok, r1lo_ok, 2 * b + 2)

        @block.scalar
        def _(act):
            a = nc.scalar
            act.dma_start(woff_raw[:, :], w_off.rearrange(flat)).then_inc(woff_in, 16)
            act.dma_start(wd_raw[:, :], wd.rearrange(flat)).then_inc(wd_in, 16)
            act.wait_ge(zeroed, 2)
            act.dma_start(boffc[0:OFFC, :], b_off.rearrange("(c a) -> c a", a=1)).then_inc(boff_in, 16)
            a.activation(warm[:, :], warm[:, :], ACT.Sqrt)
            act.wait_ge(zeroed, 3)
            act.wait_ge(woff_t, 1)
            a.activation(woffT[:, :, 0:OFFC], PS[:, 0, 0:TAPS * OFFC].rearrange("p (k o) -> p k o", k=TAPS),
                         ACT.Copy).then_inc(woff_hi, 1)

            def root(n, b):
                act.wait_ge(gn_var, order(n, b) + 1)
                a.activation(nsm[:, n, 3, images(n, b)], nsm[:, n, 2, images(n, b)], ACT.Sqrt).then_inc(gn_std, 1)

            def heads(n, b):
                act.wait_ge(gn_ok, order(n, b) + 1)
                a.activation(inner(xhi, b), square(xs[:, b, :]), ACT.Identity, bias=shift_of(n, b),
                             scale=scale_of(n, b)).then_inc(xhi_ok, 1)

            def whole(n, b):
                a.activation(xn[n][:, b, :], xs[:, b, :], ACT.Identity, bias=shift_of(n, b),
                             scale=scale_of(n, b)).then_inc(xn_ok, 1)

            def normalise_y(b):
                act.wait_ge(gn_ok, order(GN8, b) + 1)
                a.activation(ysb[:, b, :], ysb[:, b, :], ACT.Identity, bias=shift_of(GN8, b),
                             scale=scale_of(GN8, b)).then_inc(y_norm, 1)

            root(GN0, 0)
            heads(GN0, 0)
            whole(GN0, 0)
            for m in range(K):
                act.wait_ge(wd_t, m + 1)
                a.activation(wdhi[:, K * m:K * m + K, :], PS[:, 1 + m, 0:K * P].rearrange("p (k o) -> p k o", k=K),
                             ACT.Copy).then_inc(wd_hi, 1)
            root(GN0, 1)
            for b in range(1, B):
                heads(GN0, b)
                whole(GN0, b)

            def regroup(n):
                act.wait_ge(off_t, n + 1)
                rows = slice(n * H // 2, (n + 1) * H // 2)
                for g in range(2):
                    a.activation(omr[(g + 2) * GRP:(g + 3) * GRP, rows, :], omr[g * GRP:(g + 1) * GRP, rows, :],
                                 ACT.Copy).then_inc(off_ok, 1)

            def masks(b):
                tiles = slice(b * NT, (b + 1) * NT)
                act.wait_ge(off_ok, 4 * b + 4)
                logits = omr[:, b * H:(b + 1) * H, 2 * TAPS:OFFC].rearrange("p (t a) k -> p t k a", a=TR)
                a.activation(mask[:, tiles, :].rearrange("p t (k a) -> p t k a", a=TR), logits, ACT.Sigmoid).then_inc(mask_ok, 1)

            def row_profiles(b, step):
                v = roww[:, b * NT:(b + 1) * NT, :, :]
                if step == 0:
                    act.wait_ge(row_d, 2 * b + 2)
                    a.activation(v, v, ACT.Abs).then_inc(row_h, 1)
                else:
                    act.wait_ge(row_h, 2 * b + 1)
                    a.activation(v, v, ACT.Relu, scale=-1.0, bias=1.0).then_inc(row_h, 1)

            for s in (z_ok, y_ok):
                act.sem_inc(s, CREDIT)

            def distance(tile, par):
                act.wait_ge(hx_d, tile + 1)
                a.activation(hx[:, par, :, :], hx[:, par, :, :], ACT.Abs).then_inc(hx_a, 1)

            def hats(tile, par):
                act.wait_ge(hx_a, tile + 1)
                a.activation(hx[:, par, :, :], hx[:, par, :, :], ACT.Relu, scale=-1.0, bias=1.0).then_inc(hx_ok, 1)

            def copy_z(b, z, par, ky, bank, used):
                act.wait_ge(z_mm, b * ZPER + z + 1 + CREDIT)
                act.wait_ge(o_mm, used + CREDIT)
                a.activation(zr[:, par, ky, :, :], bank[:, 0:K * P].rearrange("p (k o) -> p k o", k=K),
                             ACT.Copy).then_inc(z_ok, 1)

            def seam(b, ky):
                for j, bank in enumerate((Z_PS[(ky + 1) % 2], ZB_PS[ky % 2])):
                    copy_z(b, 2 * ky + j, j, ky, bank, b * SLOTS - K + ky + 1 if b else 0)

            def centre_weights(i):
                act.wait_ge(tern_th, 2 * i + 2)
                a.activation(wraw[i], wraw[i], ACT.Identity, bias=tw[:, i, 13:14]).then_inc(tern_c, 1)

            for n in range(2 * B):
                act.wait_ge(off_mm, n + 1)
                if n >= 2:
                    act.wait_ge(off_sum, n - 1)
                a.activation(omt[:, n % 2, :], OFF_PS[n % 4][GRP:2 * GRP, :], ACT.Copy).then_inc(off_tail, 1)
                if n >= 1:
                    regroup(n - 1)
                if n == 4:
                    centre_weights(0)
                if n == 3:
                    masks(0)
                    for step in range(2):
                        row_profiles(0, step)
            seam(0, 0)
            regroup(2 * B - 1)
            distance(0, 0)
            hats(0, 0)
            seam(0, 1)
            seam(0, 2)

            def copy_weights(m):
                for i in (2 * m, 2 * m + 1):
                    act.wait_ge(q_t, i + 1)
                    a.activation((q1, q2)[i // K][:, i % K * K:i % K * K + K, :],
                                 ZB_PS[i % 2][:, 0:K * P].rearrange("p (k o) -> p k o", k=K), ACT.Copy).then_inc(q_ok, 1)

            def meanwhile(b, final, u):
                if b == 0 and not final:
                    if u in (0, 2, 4):
                        masks(1 + u // 2)
                    if u in (1, 3):
                        row_profiles(1, u // 2)
                    if u == 5:
                        centre_weights(1)
                if b == 1 and not final and u in (1, 3, 5):
                    copy_weights(u // 2)
                if b == 0 and final and u == 0:
                    a.activation(warm[:, :], warm[:, :], ACT.Sqrt)
                if b == 0 and final and u in (1, 3):
                    row_profiles(2, u // 2)
                if b == 1 and not final and u in (0, 2):
                    row_profiles(3, u // 2)
                if b >= 2 and not final and u == 4:
                    root(GN1, b - 2)
                if b and not final and u == 5:
                    root(GN8, b - 1)
                if b and final:
                    if u == 0:
                        normalise_y(b - 1)
                    if u == 1 and b >= 2:
                        heads(GN1, b - 2)
                    if u == 2 and b >= 2:
                        whole(GN1, b - 2)

            act.wait_ge(vec_in, 7 * 16)
            act.wait_ge(far_ok, 1)
            near = act.value_load(fari[0:1, 0:1], min_val=0, max_val=1)
            with act.If(near == 1):
                def pair(b, i, first=False, final=False):
                    for par in range(2):
                        for ky in range(K):
                            u = K * par + ky
                            if not (final and par == 1):
                                copy_z(b, 6 * i + u + 6, par, ky, Z_PS[u % 2], b * SLOTS + 6 * i + u + 1)
                            elif b < B - 1:
                                seam(b + 1, ky)
                            if ky and not (final and b == B - 1):
                                (distance, hats)[ky - 1](b * NT + 2 * i + par + 2, par)
                            if first or final:
                                meanwhile(b, final, u)
                        act.wait_ge(o_mm, b * SLOTS + 6 * i + K * par + K + CREDIT)
                        a.activation(ysb[:, b, bass.ds((2 * i + par) * P, P)], O_PS[par][:, 0:P], ACT.Identity,
                                     bias=v_bias).then_inc(y_ok, 1)

                distance(1, 1)
                hats(1, 1)
                for b in range(B):
                    pair(b, 0, first=True)
                    with act.Fori(1, NT // 2 - 1) as i:
                        pair(b, i)
                    pair(b, NT // 2 - 1, final=True)
                act.wait_ge(y_ok, B * NT + CREDIT)
                act.sem_inc(y_done, 1)
            with act.Else():
                distance(1, 1)
                hats(1, 1)
                centre_weights(1)
                for b in range(1, B):
                    masks(b)
                with act.Fori(0, B) as b:
                    with act.Fori(0, TAPS) as k:
                        it = b * TAPS + k
                        for j in range(NT):
                            act.wait_ge(z_mm, it * NT + j + 1 + PRIMED)
                            act.wait_ge(o_mm, it * NT + CREDIT)
                            a.activation(zany[:, j * P:(j + 1) * P], Z_PS[j % 2][:, 0:P], ACT.Copy).then_inc(z_ok, 1)
                act.wait_ge(y_ok, TAPS * B * NT + CREDIT)
                act.sem_inc(y_done, 1)

                for n, b in IN_LOOP:
                    root(n, b)
                    if n == GN8:
                        normalise_y(b)
                    else:
                        heads(n, b)
                        whole(n, b)
                for m in range(K):
                    copy_weights(m)

            root(GN1, B - 2)
            root(GN8, B - 1)
            normalise_y(B - 1)
            heads(GN1, B - 2)
            whole(GN1, B - 2)
            root(GN1, B - 1)
            heads(GN1, B - 1)
            whole(GN1, B - 1)
            root(BN1, 0)
            act.wait_ge(gn_ok, order(BN1, 0) + 1)
            for n in range(2 * B):
                for dst, src, done in ((chunk_rows(xhi, n), square(PS[:, n, :]), r1hi_ok), (chunk(r1, n), PS[:, n, :], r1_ok)):
                    a.activation(dst, src, ACT.Relu, bias=shift_of(BN1, 0), scale=scale_of(BN1, 0)).then_inc(done, 1)
            root(BN2, 0)
            act.wait_ge(gn_ok, order(BN2, 0) + 1)
            for n in POOL_CHUNKS:
                a.activation(chunk(ysb, n), PS[:, n, :], ACT.Identity, bias=shift_of(BN2, 0),
                             scale=scale_of(BN2, 0)).then_inc(f_act, 1)
            for m, n in enumerate(POOL_CHUNKS):
                act.wait_ge(f_sum, m + 1)
                a.activation(chunk(ysb, n), chunk(ysb, n), ACT.Relu).then_inc(f_relu, 1)

        @block.vector
        def _(dve):
            d = nc.vector
            steps = [0]

            def link(ins):
                steps[0] += 1
                ins.then_inc(dch, 1)
                dve.wait_ge(dch, steps[0])

            d.memset(warm[:, :], 0.0).then_inc(zeroed, 1)
            d.memset(boffc[:, :], 0.0).then_inc(zeroed, 1)
            d.memset(woffT[:, :, :].bitcast(F32), 0.0).then_inc(zeroed, 1)

            def small(n, b):
                return [nsm[:, n, i, images(n, b)] for i in range(10)]

            def square_plus(out, a_, c_, scratch):
                if a_.shape[-1] == 1:
                    return d.scalar_tensor_tensor(out=out, in0=a_, scalar=a_, in1=c_, op0=ALU.mult, op1=ALU.add)
                link(d.tensor_tensor(scratch, a_, a_, ALU.mult))
                return d.tensor_tensor(out, scratch, c_, ALU.add)

            def deviation(n, b):
                s = small(n, b)
                dve.wait_ge(gn_mean, order(n, b) + 1)
                d.tensor_scalar(s[4], group_sums(n, b)[0], -1.0, None, ALU.mult)
                link(d.tensor_tensor(s[0], mv[:, n, images(n, b), 0], group_sums(n, b)[0], ALU.subtract))
                square_plus(s[1], s[0], mv[:, n, images(n, b), 1], s[3]).then_inc(gn_dev, 1)

            def variance(n, b):
                s = small(n, b)
                if n in (BN1, BN2):
                    var = mv[:, n, 0:1, 1]
                    d.tensor_scalar(s[4], mv[:, n, 0:1, 0], -1.0, None, ALU.mult)
                else:
                    dve.wait_ge(gn_msq, order(n, b) + 1)
                    var = group_sums(n, b)[1]
                d.tensor_scalar(s[2], var, EPS, None, ALU.add).then_inc(gn_var, 1)

            def scale_shift(n, b, weight=None, shift=None):
                s = small(n, b)
                dve.wait_ge(gn_std, order(n, b) + 1)
                link(d.reciprocal(s[5], s[3]))
                link(d.scalar_tensor_tensor(out=s[6], in0=s[5], scalar=-0.5, in1=s[5], op0=ALU.mult, op1=ALU.mult))
                link(d.tensor_tensor(s[6], s[6], s[2], ALU.mult))
                link(d.scalar_tensor_tensor(out=s[8], in0=s[6], scalar=1.5, in1=s[5], op0=ALU.add, op1=ALU.mult))
                if weight is None:
                    d.tensor_tensor(s[9], s[4], s[8], ALU.mult).then_inc(gn_ok, 1)
                else:
                    link(d.tensor_scalar(s[8], s[8], weight, None, ALU.mult))
                    d.scalar_tensor_tensor(out=s[9], in0=s[4], scalar=s[8], in1=shift, op0=ALU.mult,
                                           op1=ALU.add).then_inc(gn_ok, 1)

            def half_stats(n, b, h, src):
                return d.bn_stats(st[:, n, 2 * b + h, :], src[:, b, h * BIG:(h + 1) * BIG])

            def image_stats(n, b, src, last=True, halves=(0, 1)):
                for h in halves:
                    ins = half_stats(n, b, h, src)
                link(ins)
                ins = d.bn_aggr(mv[:, n, b, :], st[:, n, 2 * b:2 * b + 2, :])
                if last:
                    ins.then_inc(gn_in, 1)

            def stats_x1(b):
                dve.wait_ge(x1_ok, 2 * b + 2)
                image_stats(GN1, b, xs)

            def tails(n, b):
                dve.wait_ge(xn_ok, (B if n == GN1 else 0) + b + 1)
                d.tensor_tensor(inner(xlo, b), square(xn[n][:, b, :]), inner(xhi, b), ALU.subtract).then_inc(xlo_ok, 1)

            def weights_max(i):
                dve.wait_ge((w1_in, w2_in)[i], 16)
                d.tensor_reduce(tw[:, i, 1:2], wraw[i], AX.X, ALU.max)

            def weights_min(i):
                d.tensor_reduce(tw[:, i, 3:4], wraw[i], AX.X, ALU.min).then_inc(tern_min, 1)

            def weights_sum(i):
                dve.wait_ge(tern_fold, FOLDS * (i + 1))
                d.tensor_reduce(tw[:, i, 0:1], fold[i][:, 0:C * TAPS >> FOLDS], AX.X, ALU.add)
                dve.wait_ge(tern_min, i + 1)
                d.tensor_scalar(tw[:, i, 2:3], tw[:, i, 3:4], -1.0, None, ALU.mult).then_inc(tern_in, 1)

            def below(i):
                dve.wait_ge(tern_c, i + 1)
                if i:
                    dve.wait_ge(tern_ok, i)
                link(d.tensor_scalar(wscr, wraw[i], tw[:, i, 11:12], None, ALU.is_lt))

            def ternary(i):
                d.scalar_tensor_tensor(out=wraw[i], in0=wraw[i], scalar=tw[:, i, 12:13], in1=wscr, op0=ALU.is_gt,
                                       op1=ALU.subtract).then_inc(tern_ok, 1)

            def largest(b):
                dve.wait_ge(off_ok, 4 * b + 4)
                ins = d.tensor_reduce(far[:, b:b + 1], omr[:, b * H:(b + 1) * H, 0:2 * TAPS], AX.XY, ALU.max,
                                      apply_absolute_value=True)
                if b == B - 1:
                    link(ins)
                    d.tensor_reduce(far[:, B:B + 1], far[:, 0:B], AX.X, ALU.max).then_inc(far_in, 1)

            def masked(b):
                tiles = slice(b * NT, (b + 1) * NT)
                dve.wait_ge(row_h, 2 * b + 2)
                dve.wait_ge(mask_ok, b + 1)
                d.tensor_tensor(roww[:, tiles, :, :], roww[:, tiles, :, :],
                                mask[:, tiles, :].unsqueeze(3).to_broadcast([P, NT, TAPS * TR, 2]), ALU.mult).then_inc(row_ok, 1)

            dve.wait_ge(x_in[0], 16)
            image_stats(GN0, 0, xs)
            deviation(GN0, 0)
            variance(GN0, 0)
            scale_shift(GN0, 0)
            dve.wait_ge(woff_hi, 1)
            d.tensor_tensor(woffT[:, :, GRP:GRP + OFFC], PS[:, 0, 0:TAPS * OFFC].rearrange("p (k o) -> p k o", k=TAPS),
                            woffT[:, :, 0:OFFC], ALU.subtract).then_inc(woff_ok, 1)
            dve.wait_ge(x_in[1], 16)
            image_stats(GN0, 1, xs, last=False)
            dve.wait_ge(consts, 6)
            dve.wait_ge(by_i, 2)
            d.tensor_scalar(ci[:, 1:2], ci[:, 0:1], 5, None, ALU.logical_shift_right)
            link(d.tensor_scalar(ci[:, 2:3], ci[:, 0:1], W - 1, None, ALU.bitwise_and))
            d.tensor_copy(byf, byi.bitcast(I32))
            d.tensor_copy(rbf, rbi.bitcast(I32))
            d.tensor_copy(bxf[:, :], bxi[:, :])
            d.tensor_copy(colf[:, :], coli[:, :])
            link(d.tensor_copy(cf[:, 1:3], ci[:, 1:3]))
            d.tensor_scalar(bxf[:, :], bxf[:, :], cf[:, 2:3], None, ALU.add)
            d.tensor_scalar(rowj[:, :], colf[:, 0:NT], float(TR), cf[:, 1:2], ALU.mult, ALU.add)
            link(d.tensor_scalar(rbf, rbf, cf[:, 1:2], None, ALU.add))
            d.tensor_scalar(rbf2, rbf, float(TR), None, ALU.add).then_inc(base_ok, 1)
            tails(GN0, 0)
            for b in (2, 3):
                dve.wait_ge(x_in[b], 16)
                image_stats(GN0, b, xs, last=b == B - 1)
            weights_max(0)
            deviation(GN0, 1)
            weights_min(0)
            variance(GN0, 1)
            scale_shift(GN0, 1)
            for m in range(K):
                dve.wait_ge(wd_hi, m + 1)
                d.tensor_tensor(wdlo[:, K * m:K * m + K, :], PS[:, 1 + m, 0:K * P].rearrange("p (k o) -> p k o", k=K),
                                wdhi[:, K * m:K * m + K, :], ALU.subtract).then_inc(wd_ok, 1)
            weights_sum(0)
            tails(GN0, 1)
            weights_max(1)
            tails(GN0, 2)
            weights_min(1)
            tails(GN0, 3)
            weights_sum(1)

            def window(b, j, par):
                for part, src in enumerate((xhi, xlo)):
                    d.tensor_copy(xwin[:, part, par, :, :],
                                  src[:, bass.ds(b * ROWS + j * TR, K + TR - 1), 1:1 + W]).then_inc(xw_ok, 1)

            def columns(tile, par):
                d.tensor_tensor(hx[:, par, :, :],
                                px[:, bass.ds(tile, 1), :].rearrange("p t n -> p (t n)").unsqueeze(2)
                                .to_broadcast([P, TAPS * TR, W]),
                                colf[:, :].unsqueeze(1).to_broadcast([P, TAPS * TR, W]), ALU.subtract).then_inc(hx_d, 1)

            dve.wait_ge(boff_in, 16)
            for n in range(2 * B):
                dve.wait_ge(off_tail, n + 1)
                if n >= 2:
                    dve.wait_ge(off_t, n - 1)
                d.scalar_tensor_tensor(out=omh[:, n % 2, :], in0=OFF_PS[n % 4][0:GRP, :], scalar=boffc[:, 0:1],
                                       in1=omt[:, n % 2, :], op0=ALU.add, op1=ALU.add).then_inc(off_sum, 1)
                dve.wait_ge(off_sum, n + 1)
                for g in range(2):
                    ins = d.transpose(omr[g * GRP:(g + 1) * GRP, n * H // 2:(n + 1) * H // 2, :].rearrange("p h c -> p (h c)"),
                                      omh[:, n % 2, :])
                ins.then_inc(off_t, 1)
                if n in (2, 4):
                    largest(n // 2 - 1)
                if n == 3:
                    masked(0)
                if n == 4:
                    window(0, 0, 0)
                    window(0, 1, 1)
            dve.wait_ge(pos_ok, 2)
            columns(0, 0)
            largest(B - 2)
            largest(B - 1)
            dve.wait_ge(z_mm, 5 + CREDIT)
            window(0, 2, 0)
            dve.wait_ge(far_red, 1)
            d.tensor_scalar(fari[0:1, 0:1], far[0:1, B + 1:B + 2], float(REACH), None, ALU.is_le).then_inc(far_ok, 1)
            columns(1, 1)

            dve.sem_inc(s_ok, CREDIT)
            dve.wait_ge(far_ok, 1)

            def normalise_sample(b):
                image_stats(GN8, b, ysb)
                deviation(GN8, b)
                variance(GN8, b)
                scale_shift(GN8, b, v_gamma, v_beta)

            def normalise_x1(b):
                stats_x1(b)
                deviation(GN1, b)
                variance(GN1, b)
                scale_shift(GN1, b)

            before = steps[0]
            near = dve.value_load(fari[0:1, 0:1], min_val=0, max_val=1)
            with dve.If(near == 1):
                def turn(b, s, par):
                    dve.wait_ge(v_ok, b * SLOTS + s + 1 + CREDIT)
                    dve.wait_ge(o_mm, b * SLOTS + s - 1 + CREDIT)
                    flat_ = "p n r w -> p (n r w)"
                    d.transpose(sq[:, par, :, :, :].rearrange(flat_), vt[:, par, :, :, :].rearrange(flat_)).then_inc(s_ok, 1)

                def meanwhile(b, final, u):
                    if b == 0:
                        placed = {(False, 0): (below, 0), (False, 1): (ternary, 0),
                                  (True, 0): (below, 1), (True, 1): (ternary, 1), (True, 3): (masked, 1)}
                        if final and u == 4:
                            dve.wait_ge(y_ok, b * NT + NT // 2 + CREDIT)
                            half_stats(GN8, b, 0, ysb)
                        if (final, u) in placed:
                            part, i = placed[final, u]
                            part(i)
                    elif not final:
                        if u == 4 and b == B - 1:
                            tails(GN1, b - 3)
                        if u == 0 and b >= 2:
                            stats_x1(b - 2)
                        if u == 1:
                            dve.wait_ge(y_ok, b * NT + CREDIT)
                            image_stats(GN8, b - 1, ysb, halves=(1,))
                        for n, img, at in ((GN1, b - 2, 2), (GN8, b - 1, 3)):
                            if img >= 0 and u == at:
                                deviation(n, img)
                            if img >= 0 and u == at + 2:
                                variance(n, img)
                    else:
                        if b == 1 and u in (0, 4):
                            masked(2 + u // 4)
                        if u == 0 and b >= 2:
                            scale_shift(GN1, b - 2)
                        if u == 0:
                            scale_shift(GN8, b - 1, v_gamma, v_beta)
                        if u == 3:
                            dve.wait_ge(y_ok, b * NT + NT // 2 + CREDIT)
                            half_stats(GN8, b, 0, ysb)

                def pair(b, i, first=False, final=False):
                    for par in range(2):
                        for ky in range(K):
                            turn(b, 6 * i + K * par + ky, (par + ky) % 2)
                            if first or final:
                                meanwhile(b, final, K * par + ky)
                        if not (final and b == B - 1):
                            columns(b * NT + 2 * i + par + 2, par)
                        if not final:
                            dve.wait_ge(z_mm, b * ZPER + 6 * i + K * par + 2 * K + CREDIT)
                            window(b, 2 * i + par + 3, 1 - par)
                        elif b < B - 1:
                            if par == 0:
                                dve.wait_ge(z_mm, (b + 1) * ZPER + CREDIT)
                                window(b + 1, 0, 0)
                                window(b + 1, 1, 1)
                            else:
                                dve.wait_ge(z_mm, (b + 1) * ZPER + 5 + CREDIT)
                                window(b + 1, 2, 0)

                for b in range(B):
                    pair(b, 0, first=True)
                    with dve.Fori(1, NT // 2 - 1) as i:
                        pair(b, i)
                    pair(b, NT // 2 - 1, final=True)
            with dve.Else():
                steps[0] = before
                dve.wait_ge(hx_ok, 2)
                dve.wait_ge(mask_ok, B)
                dve.wait_ge(pos_ok, 2 * B)
                dve.wait_ge(vec_in, 7 * 16)
                d.memset(ysb[:, :, :], 0.0).then_inc(any_ok, 1)
                dve.wait_ge(any_ok, 1)
                d.tensor_scalar(ysb[:, :, :], ysb[:, :, :], v_bias, None, ALU.add).then_inc(any_ok, 1)
                dve.wait_ge(any_ok, 2)
                hf = hx[:, :, :, :].rearrange("p a n w -> p (a n w)")
                cols = [hf[:, m * NT * P:(m + 1) * NT * P].rearrange("p (n w) -> p n w", w=W) for m in range(2)]
                rows = [rowany[:, m, :, :] for m in range(2)]

                with dve.Fori(0, B) as b:
                    with dve.Fori(0, TAPS) as k:
                        it = b * TAPS + k
                        done = [0]

                        def step(ins):
                            done[0] += 1
                            ins.then_inc(any_ok, 1)
                            dve.wait_ge(any_ok, it * 7 + 2 + done[0])

                        for j in range(NT):
                            dve.wait_ge(z_mm, it * NT + j - 1 + PRIMED)
                            for part, src in enumerate((xhi, xlo)):
                                d.tensor_copy(xwin[:, part, j % 2, 0:TR, :],
                                              src[:, bass.ds(b * ROWS + TOP + j * TR, TR), 1:1 + W]).then_inc(xw_ok, 1)
                        at = (slice(None), bass.ds(b * NT, NT), bass.ds(k * TR, TR))
                        for m, pos, n in ((cols, px, W), (rows, py, NT)):
                            p_ = pos[at].unsqueeze(3).to_broadcast([P, NT, TR, n])
                            q_ = (colf[:, :] if n == W else rowj[:, :]).unsqueeze(1).unsqueeze(1).to_broadcast([P, NT, TR, n])
                            m0, m1 = (x_.rearrange("p (t a) w -> p t a w", a=TR) for x_ in m)
                            d.tensor_tensor(m0, p_, q_, ALU.subtract)
                            step(d.tensor_tensor(m1, q_, p_, ALU.subtract))
                            step(d.tensor_tensor(m[0], m[0], m[1], ALU.max))
                            step(d.tensor_scalar(m[0], m[0], 1.0, -1.0, ALU.min, ALU.add))
                        step(d.tensor_tensor(rows[0].rearrange("p (t a) w -> p t a w", a=TR),
                                             rows[0].rearrange("p (t a) w -> p t a w", a=TR),
                                             mask[at].unsqueeze(3).to_broadcast([P, NT, TR, NT]), ALU.mult))
                        for pt in range(NT):
                            for half in range(2):
                                n = (it * NT + pt) * 2 + half
                                r_ = rows[0][:, pt * TR:(pt + 1) * TR, 4 * half:4 * half + 4].rearrange("p a j -> p j a")
                                c_ = cols[0][:, pt * TR:(pt + 1) * TR, :]
                                d.tensor_tensor(sany(vt, half).rearrange("p j (a w) -> p j a w", w=W),
                                                r_.unsqueeze(3).to_broadcast([P, 4, TR, W]),
                                                c_.unsqueeze(1).to_broadcast([P, 4, TR, W]), ALU.mult).then_inc(v_ok, 1)
                                dve.wait_ge(v_ok, n + 1 + CREDIT)
                                dve.wait_ge(o_mm, it * NT + pt + CREDIT)
                                d.transpose(sany(sq, half).rearrange("p j n -> p (j n)"),
                                            sany(vt, half).rearrange("p j n -> p (j n)")).then_inc(s_ok, 1)
                            dve.wait_ge(o_mm, it * NT + pt + 1 + CREDIT)
                            y = ysb[:, bass.ds(b, 1), pt * P:(pt + 1) * P].rearrange("p a n -> p (a n)")
                            d.tensor_tensor(y, y, O_PS[pt % 2][:, 0:P], ALU.add).then_inc(y_ok, 1)

                dve.wait_ge(y_done, 1)
                half_stats(GN8, B - 1, 0, ysb)
                for b in range(B - 1):
                    normalise_sample(b)
                    if b < B - 2:
                        normalise_x1(b)
                    if b == 0:
                        tails(GN1, b)
                for i in range(2):
                    below(i)
                    ternary(i)

            dve.wait_ge(y_done, 1)
            stats_x1(B - 2)
            image_stats(GN8, B - 1, ysb, halves=(1,))
            tails(GN1, B - 3)
            late = ((GN1, B - 2), (GN8, B - 1))
            for n, b in late:
                deviation(n, b)
            for n, b in late:
                variance(n, b)
            scale_shift(GN1, B - 2)
            scale_shift(GN8, B - 1, v_gamma, v_beta)
            dve.wait_ge(y_norm, B)
            d.tensor_tensor(xs[:, B - 1, :], xs[:, B - 1, :], ysb[:, B - 1, :], ALU.add).then_inc(x1_ok, 2)
            stats_x1(B - 1)
            tails(GN1, B - 2)
            deviation(GN1, B - 1)
            variance(GN1, B - 1)
            scale_shift(GN1, B - 1)
            tails(GN1, B - 1)

            def conv_stats(n, done):
                for m in range(2 * B):
                    dve.wait_ge(done, m + 1)
                    ins = d.bn_stats(st[:, n, m, :], PS[:, m, :])
                link(ins)
                link(d.bn_aggr(mv[:, n, 0, :], st[:, n, :, :]))

            conv_stats(BN1, c1_mm)
            variance(BN1, 0)
            scale_shift(BN1, 0, v_g1, v_be1)
            for n in range(2 * B):
                dve.wait_ge(r1_ok, n + 1)
                d.tensor_tensor(chunk_rows(xlo, n), square(chunk(r1, n)), chunk_rows(xhi, n), ALU.subtract).then_inc(r1lo_ok, 1)
            conv_stats(BN2, c2_mm)
            variance(BN2, 0)
            scale_shift(BN2, 0, v_g2, v_be2)

            dve.wait_ge(gn_ok, order(BN2, 0) + 1)

            def scaled(m):
                n = DVE_CHUNKS[m]
                dve.wait_ge(rx_ok, m + 1)
                d.scalar_tensor_tensor(out=chunk(ysb, n), in0=PS[:, n, :], scalar=scale_of(BN2, 0),
                                       in1=chunk(ysb, n), op0=ALU.mult, op1=ALU.add).then_inc(f_scaled, 1)

            scaled(0)
            for m in range(B):
                if m < B - 1:
                    scaled(m + 1)
                n = DVE_CHUNKS[m]
                dve.wait_ge(f_scaled, m + 1)
                d.scalar_tensor_tensor(out=chunk(ysb, n), in0=chunk(ysb, n), scalar=shift_of(BN2, 0),
                                       in1=chunk(xs, n), op0=ALU.add, op1=ALU.max).then_inc(out_ok[n], 1)
                if m:
                    n = POOL_CHUNKS[m - 1]
                    dve.wait_ge(f_relu, m)
                    d.tensor_tensor(chunk(ysb, n), chunk(ysb, n), chunk(xs, n), ALU.add).then_inc(out_ok[n], 1)


_INS = ["x", "L0_conv_w_off", "L0_conv_b_off", "L0_conv_weight", "L0_conv_bias", "L0_conv_gamma", "L0_conv_beta",
        "L1_conv_w1", "L1_conv_gamma1", "L1_conv_beta1", "L1_conv_w2", "L1_conv_gamma2", "L1_conv_beta2"]


def kernel(**inputs):
    import numpy as np
    import concourse.bacc as bacc
    from concourse.bass_utils import run_bass_kernel_spmd

    nc = bacc.Bacc("TRN2", target_bir_lowering=False, num_devices=1)
    arrays, args = {}, []
    for name in _INS:
        arrays[f"in_{name}"] = a = np.ascontiguousarray(inputs[name])
        args.append(nc.dram_tensor(f"in_{name}", a.shape, mybir.dt.from_np(a.dtype), kind="ExternalInput").ap())
    out = nc.dram_tensor("out", (B, C, H, W), F32, kind="ExternalOutput").ap()
    build(nc, *args, out)
    r = run_bass_kernel_spmd(nc, [arrays], core_ids=[0])
    return r.results[0]["out"]
```
